# Optimizing a Trainium2 kernel written in Bass

```python
import numpy as np
import jax
import jax.numpy as jnp

def _softmax(x, axis=-1):
    return jax.nn.softmax(x, axis=axis)

def _gelu(x):
    return jax.nn.gelu(x, approximate=True)

def _silu(x):
    return jax.nn.silu(x)

def _sigmoid(x):
    return jax.nn.sigmoid(x)

def _layernorm(x, axis=-1, eps=1e-05):
    m = jnp.mean(x, axis=axis, keepdims=True)
    v = jnp.var(x, axis=axis, keepdims=True)
    return (x - m) / jnp.sqrt(v + eps)

def _scatter_add(tgt, idx, src, axis=0):
    return tgt.at[idx].add(src)

def _segment_sum(src, seg, n):
    return jax.ops.segment_sum(src, seg, n)
kernel_name = 'mk_conv_preact_d1_conv_nchw256_r2_aa4662'

def setup_inputs(seed: int=0):
    np.random.seed(seed)
    _w = jnp.asarray

    def _rec_inputs():
        import jax
        import jax.numpy as jnp
        _gk = jax.random.key(seed)
        x = -8.268e-05 + 0.9999 * jax.random.normal(jax.random.fold_in(_gk, 1), (32, 128, 56, 56), jnp.float32)
        return x
    x = _rec_inputs()

    def _L0_conv_setup():
        import jax, jax.numpy as jnp
        import numpy as np
        EPS = 0.0001

        def _zca_forward(x, weight, bias, groups=16):
            N, C, H, W = x.shape
            G = groups
            c = C // G
            M = N * H * W
            xf = jnp.transpose(x, (1, 0, 2, 3)).reshape(C, M)
            mu = jnp.mean(xf, axis=1, keepdims=True)
            xc = xf - mu
            xg = xc.reshape(G, c, M)
            cov = jnp.einsum('gim,gjm->gij', xg, xg) / M
            cov = cov + EPS * jnp.eye(c, dtype=x.dtype)
            e, v = jnp.linalg.eigh(cov)
            inv_sqrt = jax.lax.rsqrt(e)
            proj = jnp.einsum('gik,gk,gjk->gij', v, inv_sqrt, v)
            xw = jnp.einsum('gij,gjm->gim', proj, xg).reshape(C, M)
            out = xw * weight + bias
            return jnp.transpose(out.reshape(C, N, H, W), (1, 0, 2, 3))
        key = jax.random.key(seed)
        k1, k2 = jax.random.split(key)
        N, C, H, W = (32, 128, 56, 56)
        x = jax.random.normal(k1, (N, C, H, W), dtype=jnp.float32)
        weight = jax.random.uniform(k2, (C, 1), dtype=jnp.float32)
        bias = jnp.zeros((C, 1), dtype=jnp.float32)
        return {'x': x, 'weight': weight, 'bias': bias}
    _L0_conv_all = _L0_conv_setup()
    _L0_conv_in = {k: v for k, v in _L0_conv_all.items() if k in ('weight', 'bias')}
    del _L0_conv_all
    return {'x': x, 'L0_conv_weight': _L0_conv_in['weight'], 'L0_conv_bias': _L0_conv_in['bias']}

def reference(x, L0_conv_weight, L0_conv_bias):
    import jax
    import jax.numpy as jnp

    def _L0_conv_ref(x, weight, bias):
        import jax, jax.numpy as jnp
        import numpy as np
        EPS = 0.0001

        def _zca_forward(x, weight, bias, groups=16):
            N, C, H, W = x.shape
            G = groups
            c = C // G
            M = N * H * W
            xf = jnp.transpose(x, (1, 0, 2, 3)).reshape(C, M)
            mu = jnp.mean(xf, axis=1, keepdims=True)
            xc = xf - mu
            xg = xc.reshape(G, c, M)
            cov = jnp.einsum('gim,gjm->gij', xg, xg) / M
            cov = cov + EPS * jnp.eye(c, dtype=x.dtype)
            e, v = jnp.linalg.eigh(cov)
            inv_sqrt = jax.lax.rsqrt(e)
            proj = jnp.einsum('gik,gk,gjk->gij', v, inv_sqrt, v)
            xw = jnp.einsum('gij,gjm->gim', proj, xg).reshape(C, M)
            out = xw * weight + bias
            return jnp.transpose(out.reshape(C, N, H, W), (1, 0, 2, 3))
        return _zca_forward(x, weight, bias)

    def _gn(v, G=32, eps=1e-05):
        B_, C_, H_, W_ = v.shape
        g = v.reshape(B_, G, C_ // G, H_, W_)
        m = jnp.mean(g, axis=(2, 3, 4), keepdims=True)
        s = jnp.var(g, axis=(2, 3, 4), keepdims=True)
        return ((g - m) / jnp.sqrt(s + eps)).reshape(v.shape)

    def _ln_c(v, eps=1e-06):
        m = jnp.mean(v, axis=1, keepdims=True)
        s = jnp.var(v, axis=1, keepdims=True)
        return (v - m) / jnp.sqrt(s + eps)

    def _ln_t(v, eps=1e-05):
        m = jnp.mean(v, axis=-1, keepdims=True)
        s = jnp.var(v, axis=-1, keepdims=True)
        return (v - m) / jnp.sqrt(s + eps)

    def _to_tokens(v):
        B_, C_, H_, W_ = v.shape
        return v.reshape(B_, C_, H_ * W_).transpose(0, 2, 1)

    def _from_tokens(t, like):
        B_, C_, H_, W_ = like.shape
        return t.transpose(0, 2, 1).reshape(B_, C_, H_, W_)
    x = x + _L0_conv_ref(_gn(x), L0_conv_weight, L0_conv_bias)
    return x

_drawn_inputs = setup_inputs


def setup_inputs(seed=0):
    import zlib

    import numpy as np

    out = dict(_drawn_inputs(seed))
    spreads = {'L0_conv_bias': (0.0, 0.1)}
    factors = {}
    for name, (base, spread) in spreads.items():
        noise = np.random.default_rng([zlib.crc32(name.encode()), seed]).standard_normal(out[name].shape)
        drawn = base * np.exp(spread * noise) if base else spread * noise
        out[name] = jnp.asarray(drawn.astype(out[name].dtype))
    for name, factor in factors.items():
        out[name] = (out[name] * factor).astype(out[name].dtype)
    return out
```

```python
from contextlib import ExitStack

import numpy as np

import concourse.bass as bass
from concourse import mybir

ALU = mybir.AluOpType
ACT = mybir.ActivationFunctionType
AX = mybir.AxisListType
F32 = mybir.dt.float32
F16 = mybir.dt.float16

P = 128
N, C, HW = 32, 128, 56 * 56
CG = 8
GROUPS = C // CG
GN = 4
TILES = N * CG // P
SAMPLES = N // TILES
RING = 3
GN_EPS, ZCA_EPS = 1e-5, 1e-4
Y_SCALE = 256.0
TRACE = 8.002

BN = 448
BN_CHUNKS = HW // BN
HALF = HW // 2
QUARTER = HW // 4
APPLY = 392
APPLY_CHUNKS = TILES * HW // APPLY
PAIRS = APPLY_CHUNKS // 2
REST = HW % P
QUADS = TILES * (HW // (4 * P)) + 1
QT = HW // (4 * P)
HALF_SLOTS = 32

POLY = [(8.36654954, -24.69831088, 18.30331604), (4.01349494, -2.9844421, 0.56468456),
        (3.43047102, -2.56693026, 0.51741909), (2.41026743, -1.76367531, 0.42814393),
        (1.90501323, -1.2826619, 0.37803056), (1.875, -1.25, 0.375)]
ITERS = len(POLY)

HOP_MU, HOP_COV = 0, 1
def hop_p(k): return 2 if k == 0 else 3 * k + 2
def hop_m(k): return 3 * k + 1
def hop_yuz(k): return 3 if k == 0 else 3 * k + 3
HOP_T = 3 * ITERS + 1
HOP_V = HOP_T + 1
HOP_ROOT = HOP_T + 2
HOP_TURN = HOP_T + 3
HOPS = HOP_T + 4
READS = HOPS - 1
STAT_OPS = 16
TAIL_OPS = 10

STAT_MEAN_AT, STAT_VAR_AT = 17, 19
HOP_AT = [k + 1 for k in range(16)] + [18] + list(range(20, 20 + HOPS - 17))
DVE_LAG = 4
BN_AT = [1, 2, 3, 5, 6, 7, 9, 10, 11, 13, 14, 15, 17, 18]
QUAD_AT = 5

COLS = {}
_at = 0
for _name, _w in (("ident", P), ("avg", P), ("bmask", P), ("ones", P), ("gmask", 64), ("sel", CG),
                  ("e16", 2 * CG), ("expand", P), ("eps", CG), ("eye2", 2 * CG), ("eye15", CG),
                  ("bi", CG * ITERS), ("ai", CG * ITERS)):
    COLS[_name] = (_at, _at + _w)
    _at += _w
CONST_COLS = _at


def constants():
    k = np.zeros((P, CONST_COLS), np.float32)
    p = np.arange(P)

    def put(name, a):
        lo, hi = COLS[name]
        k[:a.shape[0], lo:hi] = a

    put("ident", np.eye(P))
    put("avg", (p[:, None] // GN == p[None] // GN) / GN)
    put("bmask", p[:, None] // CG == p[None] // CG)
    put("ones", np.ones((P, P)))
    ch, part = p // 2, p % 2
    put("gmask", (ch[:, None] // CG == np.arange(64)[None] // CG) * np.where(part == 1, 1.0, 2.0)[:, None]
        / (N * HW * Y_SCALE ** 2))
    put("sel", ch[:, None] % CG == np.arange(CG)[None])
    e = (p[:, None] % CG == np.arange(CG)[None]) * (2.0 / N)
    put("e16", np.concatenate([e, -2.0 * e], 1))
    put("expand", p[None] % CG == np.arange(CG)[:, None])
    eye = np.eye(CG)
    put("eps", eye * (ZCA_EPS / TRACE))
    put("eye2", np.concatenate([eye, eye], 1))
    put("eye15", 1.5 * eye)
    put("bi", np.concatenate([eye * (b / c) for a, b, c in POLY], 1))
    put("ai", np.concatenate([eye * (a / c) for a, b, c in POLY], 1))
    return k


def zca_residual(nc: bass.Bass, x: bass.AP, weight: bass.AP, bias: bass.AP, const: bass.AP, out: bass.AP):
    with ExitStack() as ctx:
        def sb(name, shape, dt=F32):
            return ctx.enter_context(nc.sbuf_tensor(name, shape, dt))

        def ps(name, shape, dt=F32):
            return ctx.enter_context(nc.psum_tensor(name, shape, dt))

        def sem(name):
            return ctx.enter_context(nc.semaphore(name))

        x_ring = sb("x_ring", [P, RING, TILES, HW])
        hl_ring = sb("hl_ring", [P, RING, TILES, HW, 2], F16)
        out_buf = sb("out_buf", [P, TILES, HW])
        hl_t = sb("hl_t", [P, 3, 4 * P, 2], F16)
        cst = sb("cst", [P, CONST_COLS])
        wb8 = sb("wb8", [CG, 2, GROUPS])
        wb = sb("wb", [P, GROUPS, 3])
        wb_g = sb("wb_g", [P, 3])
        bn = sb("bn", [P, TILES, BN_CHUNKS, 6])
        mv = sb("mv", [P, RING, TILES, 2])
        dev = sb("dev", [P, RING, TILES])
        var = sb("var", [P, TILES])
        vareps = sb("vareps", [P, TILES])
        root = sb("root", [P, TILES])
        rec = sb("rec", [P, TILES])
        heron = sb("heron", [P, TILES])
        std2 = sb("std2", [P, RING, TILES])
        r_half = sb("r_half", [P, RING, TILES])
        gmean = sb("gmean", [P, RING, TILES])
        y_mul = sb("y_mul", [P, RING, TILES])
        y_add = sb("y_add", [P, RING, TILES])
        dr = sb("dr", [P, TILES])
        drs = sb("drs", [P, 1])
        e_dr = sb("e_dr", [P, RING, 2 * CG])
        mu = sb("mu", [P, 2 * CG])
        g_masked = sb("g_masked", [P, 64])
        g_red = sb("g_red", [P, CG])
        cov = sb("cov", [CG, CG])
        mm = sb("mm", [CG, 2 * CG])
        pp = sb("pp", [CG, 2 * CG])
        yuz = sb("yuz", [CG, 3 * CG])
        tz = sb("tz", [CG, CG])
        res = sb("res", [CG, CG])
        zx = sb("zx", [CG, P])
        rmu = sb("rmu", [P, CG])
        pmu = sb("pmu", [P, 1])
        shift = sb("shift", [P, 1])
        pb = sb("pb", [P, P])
        rw = sb("rw", [P, TILES])
        a_mat = sb("a_mat", [P, TILES, P])
        a_hi = sb("a_hi", [P, RING, TILES, P], F16)
        a_lo = sb("a_lo", [P, RING, TILES, P], F16)
        fin_mul = sb("fin_mul", [P, RING, TILES])
        fin_add = sb("fin_add", [P, RING, TILES])

        ps_apply = ps("ps_apply", [P, 4, 512])
        ps_turn = ps("ps_turn", [P, 2, 512])
        ps_gram = ps("ps_gram", [P, 512])
        ps_small = ps("ps_small", [P, 512])

        x_landed = [[sem(f"x_landed_{r}_{s}") for s in range(TILES)] for r in range(RING)]
        out_stored = [sem(f"out_stored_{s}") for s in range(TILES)]
        const_landed = sem("const_landed")
        wb_product = sem("wb_product")
        wb_ready = sem("wb_ready")
        bn_done = sem("bn_done")
        stat_step = sem("stat_step")
        stat_mm = sem("stat_mm")
        root_done = sem("root_done")
        y_ready = sem("y_ready")
        h_ready = sem("h_ready")
        l_ready = sem("l_ready")
        turned = sem("turned")
        turn_copied = sem("turn_copied")
        gram_done = sem("gram_done")
        gram_masked = sem("gram_masked")
        gram_reduced = sem("gram_reduced")
        solve_mm = sem("solve_mm")
        solve_read = sem("solve_read")
        cov_copied = sem("cov_copied")
        res_copied = sem("res_copied")
        tail_step = sem("tail_step")
        a_hi_ready = sem("a_hi_ready")
        a_lo_ready = sem("a_lo_ready")
        applied = sem("applied")
        out_ready = sem("out_ready")

        passed = sem("passed")

        x_dram = x.rearrange("(s n) (g c) h w -> g s n c (h w)", s=TILES, c=CG)
        out_dram = out.rearrange("(s n) (g c) h w -> g s n c (h w)", s=TILES, c=CG)

        def k_(name, rows=P):
            lo, hi = COLS[name]
            return cst[0:rows, lo:hi]

        bi, ai = k_("bi", CG), k_("ai", CG)

        s_mu = ps_small[:, 0:16]
        s_cov = ps_small[0:CG, 16:24]
        s_mm = ps_small[0:CG, 24:40]
        s_pp = ps_small[0:CG, 40:56]
        s_yuz = ps_small[0:CG, 56:80]
        s_t = ps_small[0:CG, 80:88]
        s_v = ps_small[0:CG, 88:96]
        s_zx = ps_small[0:CG, 96:224]
        s_root = ps_small[:, 224:232]
        s_mean = ps_small[:, 232:234]
        s_var = ps_small[:, 234:236]
        s_turn = ps_small[:, 256:512]
        s_wb = ps_small[:, 128:160]

        def wait_apart(eng, semaphore, value):
            eng.wait_ge(semaphore, value)
            eng.sem_inc(passed, 1)

        def in_step(lo, i, hi=GROUPS):
            return not isinstance(i, int) or lo <= i < hi

        def pipeline(eng, step, first, loop_lo, loop_hi, last):
            for i in range(first, loop_lo):
                step(i, i % RING, (i + 1) // RING)
            with eng.Fori(0, (loop_hi - loop_lo) // RING) as trip:
                for u in range(RING):
                    step(trip * RING + (loop_lo + u), (loop_lo + u) % RING, trip + (loop_lo + u + 1) // RING)
            for i in range(loop_hi, last + 1):
                step(i, i % RING, (i + 1) // RING)

        FULL_LO, FULL_HI = 3, 3 + RING * 4
        LAST = GROUPS + 1
        assert FULL_HI + 1 <= GROUPS

        block = ctx.enter_context(nc.Block())

        @block.sync
        def _(sp):
            def load(g, slot, s):
                sp.dma_start(x_ring[:, slot, s, :], x_dram[g, s]).then_inc(x_landed[slot][s], 16)

            for s in range(TILES):
                load(0, 0, s)
            sp.dma_start(cst[:], const).then_inc(const_landed, 16)
            with nc.allow_non_contiguous_dma(reason="256 channel scalars, once"):
                sp.dma_start(wb8[:, 0, :], weight.rearrange("(g j) o -> j (g o)", j=CG)).then_inc(const_landed, 16)
                sp.dma_start(wb8[:, 1, :], bias.rearrange("(g j) o -> j (g o)", j=CG)).then_inc(const_landed, 16)
            for g in range(1, RING):
                for s in range(TILES):
                    load(g, g, s)

            def step(i, slot, visit):
                for s in range(TILES):
                    if in_step(0, i, GROUPS - RING):
                        sp.wait_ge(l_ready, 8 * i + 4 * (s + 1))
                        load(i + RING, slot, s)
                    if in_step(2, i, GROUPS + 2):
                        sp.wait_ge(out_ready, PAIRS * (i - 2) + PAIRS // 2 * (s + 1))
                        sp.dma_start(out_dram[i - 2, s], out_buf[:, s, :]).then_inc(out_stored[s], 16)

            pipeline(sp, step, 0, FULL_LO, FULL_LO + RING * 3, LAST)
            for s in range(TILES):
                sp.wait_ge(out_stored[s], 16 * GROUPS)

        @block.gpsimd
        def _(pool):
            def step(g, slot, visit):
                wait_apart(pool, stat_step, STAT_OPS * g + 13)
                for a in range(4):
                    s, px = a // 2, slice(a % 2 * HALF, (a % 2 + 1) * HALF)
                    y = x_ring[:, slot, s, px]
                    nc.gpsimd.tensor_scalar(y, y, y_mul[:, slot, s:s + 1], y_add[:, slot, s:s + 1],
                                            ALU.mult, ALU.add).then_inc(y_ready, 1)
                    wait_apart(pool, y_ready, 4 * g + a + 1)
                    if not isinstance(g, int) or g >= RING:
                        wait_apart(pool, applied, APPLY_CHUNKS * (g - RING) + APPLY_CHUNKS // TILES * (s + 1))
                    nc.gpsimd.tensor_copy(hl_ring[:, slot, s, px, 1], y).then_inc(h_ready, 1)

            pipeline(pool, step, 0, FULL_LO, FULL_HI, GROUPS - 1)

        @block.vector
        def _(dve):
            def stat(ins, g, k):
                ins.then_inc(stat_step, 1)
                wait_apart(dve, stat_step, STAT_OPS * g + k)

            def stats_rows(g, slot):
                wait_apart(dve, bn_done, TILES * BN_CHUNKS * (g + 1))
                for s in range(TILES):
                    stat(nc.vector.bn_aggr(mv[:, slot, s, :], bn[:, s].rearrange("p b k -> p (b k)")), g, s + 1)

            def stats_mean(g, slot):
                dve.wait_ge(stat_mm, 2 * g + 1)
                mean, v = mv[:, slot, :, 0], mv[:, slot, :, 1]
                stat(nc.vector.tensor_tensor(dev[:, slot], mean, s_mean, ALU.subtract), g, 3)
                stat(nc.vector.tensor_tensor(var[:], dev[:, slot], dev[:, slot], ALU.mult), g, 4)
                stat(nc.vector.tensor_tensor(var[:], var[:], v, ALU.add), g, 5)

            def stats_var(g, slot):
                dve.wait_ge(stat_mm, 2 * g + 2)
                stat(nc.vector.tensor_scalar(vareps[:], s_var, GN_EPS, None, ALU.add), g, 6)

            def stats_end(g, slot):
                dve.wait_ge(root_done, g + 1)
                stat(nc.vector.reciprocal(rec[:], root[:]), g, 7)
                stat(nc.vector.tensor_tensor(heron[:], vareps[:], rec[:], ALU.mult), g, 8)
                stat(nc.vector.tensor_tensor(std2[:, slot], heron[:], root[:], ALU.add), g, 9)
                stat(nc.vector.reciprocal(r_half[:, slot], std2[:, slot]), g, 10)
                stat(nc.vector.tensor_tensor(gmean[:, slot], mv[:, slot, :, 0], dev[:, slot], ALU.subtract), g, 11)
                stat(nc.vector.tensor_scalar(y_mul[:, slot], r_half[:, slot], 2 * Y_SCALE, None, ALU.mult), g, 12)
                stat(nc.vector.scalar_tensor_tensor(out=y_add[:, slot], in0=gmean[:, slot], scalar=-2 * Y_SCALE,
                                                    in1=r_half[:, slot], op0=ALU.mult, op1=ALU.mult), g, 13)
                stat(nc.vector.tensor_tensor(dr[:], dev[:, slot], r_half[:, slot], ALU.mult), g, 14)
                stat(nc.vector.tensor_tensor(drs[:], dr[:, 0:1], dr[:, 1:2], ALU.add), g, 15)
                stat(nc.vector.tensor_scalar(e_dr[:, slot], k_("e16"), drs[:, 0:1], None, ALU.mult), g, 16)

            def low_part(g, slot, q):
                if q % 2 == 0:
                    dve.wait_ge(h_ready, 4 * g + q // 2 + 1)
                s, px = q // 4, slice(q % 4 * QUARTER, (q % 4 + 1) * QUARTER)
                hl = hl_ring[:, slot, s, px]
                nc.vector.tensor_tensor(hl[:, :, 0], x_ring[:, slot, s, px], hl[:, :, 1],
                                        ALU.subtract).then_inc(l_ready, 1)

            def read_hop(g, slot, k):
                def tail(ins, n):
                    ins.then_inc(tail_step, 1)
                    dve.wait_ge(tail_step, TAIL_OPS * g + n)

                if k == HOP_COV:
                    dve.wait_ge(gram_done, QUADS * (g + 1))
                    nc.vector.tensor_tensor(g_masked[:], ps_gram[:, 0:64], k_("gmask"),
                                            ALU.mult).then_inc(gram_masked, 1)
                    dve.wait_ge(gram_masked, g + 1)
                    nc.vector.tensor_reduce(g_red[:], g_masked[:].rearrange("p (n i) -> p i n", i=CG),
                                            AX.X, ALU.add).then_inc(gram_reduced, 1)
                    dve.wait_ge(solve_mm, HOPS * g + k + 1)
                    nc.vector.scalar_tensor_tensor(out=cov[:], in0=s_cov, scalar=0.5 / TRACE, in1=k_("eps", CG),
                                                   op0=ALU.mult, op1=ALU.add).then_inc(cov_copied, 1)
                    dve.wait_ge(cov_copied, 2 * g + 1)
                    twice = cov[:].unsqueeze(1).broadcast_to([CG, 2, CG])
                    nc.vector.tensor_copy(mm[:].rearrange("p (a b) -> p a b", a=2), twice)
                    nc.vector.tensor_copy(yuz[:, 0:2 * CG].rearrange("p (a b) -> p a b", a=2),
                                          twice).then_inc(cov_copied, 1)
                    dve.wait_ge(cov_copied, 2 * g + 2)
                    nc.vector.tensor_copy(yuz[:, 2 * CG:], k_("eye2", CG)[:, 0:CG]).then_inc(solve_read, 1)
                for it in range(ITERS):
                    if k == hop_p(it):
                        dve.wait_ge(solve_mm, HOPS * g + k + 1)
                        nc.vector.tensor_scalar(pp[:], s_pp, POLY[it][2], None, ALU.mult).then_inc(solve_read, 1)
                if k == HOP_V:
                    dve.wait_ge(solve_mm, HOPS * g + k + 1)
                    nc.vector.scalar_tensor_tensor(out=res[:], in0=s_v, scalar=-0.5, in1=k_("eye15", CG),
                                                   op0=ALU.mult, op1=ALU.add).then_inc(res_copied, 1)
                    dve.wait_ge(res_copied, g + 1)
                    nc.vector.tensor_copy(zx[:], s_zx).then_inc(solve_read, 1)
                if k == HOP_ROOT:
                    tail(nc.vector.tensor_copy(wb_g[:], wb[:, bass.ds(g, 1), :].rearrange("p a b -> p (a b)")), 1)
                    tail(nc.vector.tensor_scalar(rw[:], r_half[:, slot], wb_g[:, 1:2], None, ALU.mult), 2)
                    dve.wait_ge(solve_mm, HOPS * g + k + 1)
                    tail(nc.vector.tensor_tensor(pb[:].rearrange("p (n c) -> p n c", c=CG),
                                                 s_root.unsqueeze(1).broadcast_to([P, SAMPLES, CG]),
                                                 k_("bmask").rearrange("p (n c) -> p n c", c=CG), ALU.mult), 3)
                    tail(nc.vector.tensor_tensor(rmu[:], s_root, mu[:, 0:CG], ALU.mult), 4)
                    for s in range(TILES):
                        ins = nc.vector.scalar_tensor_tensor(out=a_mat[:, s], in0=pb[:], scalar=rw[:, s:s + 1],
                                                             in1=k_("ident"), op0=ALU.mult, op1=ALU.add)
                        tail(ins, 5 + s)
                    nc.vector.tensor_reduce(pmu[:], rmu[:], AX.X, ALU.add).then_inc(tail_step, 1)
                    dve.wait_ge(tail_step, TAIL_OPS * g + 7)
                    tail(nc.vector.tensor_scalar(shift[:], pmu[:], wb_g[:, 0:1], wb_g[:, 2:3], ALU.mult, ALU.add), 8)
                    tail(nc.vector.tensor_scalar(fin_add[:, slot], gmean[:, slot], shift[:, 0:1], None, ALU.add), 9)
                    tail(nc.vector.tensor_scalar(fin_mul[:, slot], std2[:, slot], 0.5 / Y_SCALE, None, ALU.mult), 10)
                if k == HOP_TURN:
                    dve.wait_ge(a_hi_ready, g + 1)
                    nc.vector.tensor_tensor(a_lo[:, slot].rearrange("p s c -> p (s c)"), s_turn,
                                            a_hi[:, slot].rearrange("p s c -> p (s c)"),
                                            ALU.subtract).then_inc(solve_read, 1)

            dve.wait_ge(wb_product, 1)
            nc.vector.tensor_scalar(wb[:, :, 0], s_wb[:, 0:GROUPS], -1.0 / TRACE ** 0.5, None, ALU.mult)
            nc.vector.tensor_scalar(wb[:, :, 1], s_wb[:, 0:GROUPS], 2.0 / TRACE ** 0.5, None, ALU.mult)
            nc.vector.tensor_copy(wb[:, :, 2], s_wb[:, GROUPS:2 * GROUPS]).then_inc(wb_ready, 1)
            dve.wait_ge(wb_ready, 1)

            def step(i, slot, visit):
                for j in range(HALF_SLOTS):
                    if j % 4 == 0 and in_step(0, i):
                        low_part(i, slot, j // 4)
                    if j in BN_AT and in_step(0, i + 1):
                        c = BN_AT.index(j)
                        nslot = (slot + 1) % RING
                        s, b = divmod(c, BN_CHUNKS)
                        if b == 0:
                            dve.wait_ge(x_landed[nslot][s], 16 * (visit + 1))
                        nc.vector.bn_stats(bn[:, s, b, :],
                                           x_ring[:, nslot, s, b * BN:(b + 1) * BN]).then_inc(bn_done, 1)
                    if in_step(0, i + 1):
                        nslot = (slot + 1) % RING
                        if j == STAT_MEAN_AT + DVE_LAG - 2:
                            stats_rows(i + 1, nslot)
                        if j == STAT_MEAN_AT + DVE_LAG:
                            stats_mean(i + 1, nslot)
                        if j == STAT_VAR_AT + DVE_LAG:
                            stats_var(i + 1, nslot)
                        if j == STAT_VAR_AT + DVE_LAG + 2:
                            stats_end(i + 1, nslot)
                    if j - DVE_LAG in HOP_AT and in_step(0, i - 1):
                        read_hop(i - 1, (slot - 1) % RING, HOP_AT.index(j - DVE_LAG))

            pipeline(dve, step, -1, FULL_LO, FULL_HI, LAST)

        @block.scalar
        def _(act):
            def stats_root(g, slot):
                act.wait_ge(stat_step, STAT_OPS * g + 6)
                nc.scalar.activation(root[:], vareps[:], ACT.Sqrt).then_inc(root_done, 1)

            def copy_turned(g, slot, q):
                act.wait_ge(turned, QUADS * g + q + 1)
                before = q - 3 if q >= 3 else max(b for b in range(QUADS) if b % 3 == q % 3) - QUADS
                if before >= 0 or not isinstance(g, int) or g > 0:
                    act.wait_ge(gram_done, QUADS * g + before + 1)
                rows, cols = (P, 4 * P) if q < QUADS - 1 else (REST, TILES * P)
                dst = hl_t[0:rows, q % 3, 0:cols].rearrange("p c k -> p (c k)").bitcast(F32)
                nc.scalar.copy(dst, ps_turn[0:rows, q % 2, 0:cols]).then_inc(turn_copied, 1)

            def finish(g, slot, pair):
                s, pp_ = divmod(pair, PAIRS // TILES)
                act.wait_ge(applied, APPLY_CHUNKS * g + 2 * (pair + 1))
                if pp_ == 0:
                    act.wait_ge(tail_step, TAIL_OPS * (g + 1))
                    if not isinstance(g, int) or g > 0:
                        act.wait_ge(out_stored[s], 16 * g)
                dst = out_buf[:, s, pp_ * 2 * APPLY:(pp_ + 1) * 2 * APPLY].rearrange("p (a b) -> p a b", a=2)
                b0 = 2 * (pair % 2)
                nc.scalar.activation(dst, ps_apply[:, b0:b0 + 2, 0:APPLY], ACT.Identity,
                                     bias=fin_add[:, slot, s:s + 1],
                                     scale=fin_mul[:, slot, s:s + 1]).then_inc(out_ready, 1)

            def read_hop(g, slot, k):
                def copy(dst, src):
                    act.wait_ge(solve_mm, HOPS * g + k + 1)
                    nc.scalar.copy(dst, src).then_inc(solve_read, 1)

                if k == HOP_MU:
                    copy(mu[:], s_mu)
                for it in range(ITERS):
                    if it and k == hop_m(it):
                        copy(mm[:], s_mm)
                    if k == hop_yuz(it):
                        copy(yuz[:], s_yuz)
                if k == HOP_T:
                    copy(tz[:], s_t)
                if k == HOP_TURN:
                    act.wait_ge(solve_mm, HOPS * g + k + 1)
                    nc.scalar.copy(a_hi[:, slot].rearrange("p s c -> p (s c)"), s_turn).then_inc(a_hi_ready, 1)

            def step(i, slot, visit):
                for j in range(HALF_SLOTS):
                    if j in HOP_AT and in_step(0, i - 1):
                        read_hop(i - 1, (slot - 1) % RING, HOP_AT.index(j))
                    if j == STAT_VAR_AT + 1 and in_step(0, i + 1):
                        stats_root(i + 1, (slot + 1) % RING)
                    if j % 4 == 3 and in_step(0, i - 2):
                        finish(i - 2, (slot - 2) % RING, j // 4)
                    if j >= QUAD_AT and (j - QUAD_AT) % 2 == 0 and (j - QUAD_AT) // 2 < QUADS and in_step(0, i):
                        copy_turned(i, slot, (j - QUAD_AT) // 2)

            pipeline(act, step, -1, FULL_LO, FULL_HI, LAST)

        @block.tensor
        def _(pe):
            def product(out_, lhsT, rhs, start=True, stop=True):
                return nc.tensor.matmul(out_, lhsT, rhs, start=start, stop=stop, skip_group_check=True)

            def bank_free(g_solve, hops, g_stat, stats):
                if g_solve is not None and (not isinstance(g_solve, int) or READS * g_solve + hops > 0):
                    wait_apart(pe, solve_read, READS * g_solve + hops)
                if g_stat is not None:
                    wait_apart(pe, stat_step, STAT_OPS * g_stat + stats)

            def turn(g, slot, q):
                last = (q * 4 * P + 4 * P - 1) if q < QT else HW - 1
                if q >= QT:
                    end = min((q - QT + 1) * 4 * P, HW) if q < QUADS - 1 else HW
                    wait_apart(pe, l_ready, 8 * g + 4 + (end - 1) // QUARTER + 1)
                else:
                    wait_apart(pe, l_ready, 8 * g + last // QUARTER + 1)
                before = q - 2 if q >= 2 else max(b for b in range(QUADS) if b % 2 == q % 2) - QUADS
                if before >= 0 or not isinstance(g, int) or g > 0:
                    wait_apart(pe, turn_copied, QUADS * g + before + 1)
                for b in range(4 if q < QUADS - 1 else TILES):
                    if q < QUADS - 1:
                        s, px, n = q // QT, (q % QT * 4 + b) * P, P
                    else:
                        s, px, n = b, HW - REST, REST
                    words = hl_ring[:, slot, s, px:px + n].rearrange("p c k -> p (c k)").bitcast(F32)
                    ins = nc.tensor.transpose(ps_turn[0:n, q % 2, b * P:(b + 1) * P], words, k_("ident"))
                ins.then_inc(turned, 1)

            def gram(g, q):
                pe.wait_ge(turn_copied, QUADS * g + q + 1)
                if q == 0 and (not isinstance(g, int) or g > 0):
                    pe.wait_ge(gram_masked, g)
                full = q < QUADS - 1
                rows, blocks = (P, 4) if full else (REST, TILES)
                for b in range(blocks):
                    for half in range(2):
                        pair = hl_t[0:rows, q % 3, b * P + half * 64:b * P + half * 64 + 64]
                        first = q == 0 and b == 0 and half == 0
                        last = not full and b == blocks - 1 and half == 1
                        ins = product(ps_gram[:, 0:64], pair.rearrange("p c k -> p (c k)"), pair[:, :, 1],
                                      start=first, stop=last)
                ins.then_inc(gram_done, 1)

            def apply(g, slot, c):
                s, b = divmod(c, APPLY_CHUNKS // TILES)
                if c == 0:
                    pe.wait_ge(solve_read, READS * (g + 1))
                if c % 2 == 0 and (not isinstance(g, int) or PAIRS * g + c // 2 >= 2):
                    pe.wait_ge(out_ready, PAIRS * g + c // 2 - 1)
                hl = hl_ring[:, slot, s, b * APPLY:(b + 1) * APPLY]
                dst = ps_apply[:, c % 4, 0:APPLY]
                product(dst, a_hi[:, slot, s], hl[:, :, 1], True, False)
                product(dst, a_hi[:, slot, s], hl[:, :, 0], False, False)
                product(dst, a_lo[:, slot, s], hl[:, :, 1], False, True).then_inc(applied, 1)

            def hop(g, slot, k):
                y, u, z = yuz[:, 0:CG], yuz[:, CG:2 * CG], yuz[:, 2 * CG:]
                m, mt = mm[:, 0:CG], mm[:, CG:]
                p_, pt = pp[:, 0:CG], pp[:, CG:]
                ins = None
                if k == HOP_COV:
                    wait_apart(pe, gram_reduced, g + 1)
                if k == HOP_TURN:
                    wait_apart(pe, tail_step, TAIL_OPS * g + 6)
                if k == HOP_MU:
                    ins = product(s_mu, k_("ones"), e_dr[:, slot])
                if k == HOP_COV:
                    product(s_cov, k_("sel"), g_red[:], True, False)
                    product(s_cov, g_red[:], k_("sel"), False, False)
                    ins = product(s_cov, mu[0:1, 0:CG], mu[0:1, CG:], False, True)
                for it in range(ITERS):
                    if it and k == hop_m(it):
                        product(s_mm[:, 0:CG], z, y)
                        ins = product(s_mm[:, CG:], y, z)
                    if k == hop_p(it):
                        col = slice(it * CG, (it + 1) * CG)
                        product(s_pp, bi[:, col], mm[:], True, False)
                        product(s_pp, ai[:, col], k_("eye2", CG), False, False)
                        product(s_pp[:, 0:CG], mt, m, False, False)
                        ins = product(s_pp[:, CG:], m, mt, False, True)
                    if k == hop_yuz(it):
                        product(s_yuz[:, 0:CG], u, p_)
                        product(s_yuz[:, CG:2 * CG], p_, u)
                        ins = product(s_yuz[:, 2 * CG:], pt, z)
                if k == HOP_T:
                    ins = product(s_t, cov[:], z)
                if k == HOP_V:
                    product(s_v, z, tz[:])
                    ins = product(s_zx, z, k_("expand", CG))
                if k == HOP_ROOT:
                    ins = product(s_root, zx[:], res[:])
                if k == HOP_TURN:
                    for s in range(TILES):
                        ins = nc.tensor.transpose(s_turn[:, s * P:(s + 1) * P], a_mat[:, s], k_("ident"))
                ins.then_inc(solve_mm, 1)

            pe.wait_ge(const_landed, 48)
            product(s_wb, k_("expand", CG), wb8[:].rearrange("p a g -> p (a g)")).then_inc(wb_product, 1)
            pe.wait_ge(wb_ready, 1)

            def step(i, slot, visit):
                for j in range(HALF_SLOTS):
                    if j in HOP_AT and in_step(0, i - 1):
                        k = HOP_AT.index(j)
                        g = i - 1
                        if k == HOP_MU:
                            pe.wait_ge(stat_step, STAT_OPS * (g + 1))
                        if k != HOP_ROOT + 1:
                            bank_free(g, k, None, 0)
                        if in_step(0, i + 1) and j > STAT_MEAN_AT:
                            bank_free(None, 0, i + 1, 3 if j < STAT_VAR_AT else 6)
                        elif j < STAT_MEAN_AT and in_step(0, i):
                            bank_free(None, 0, i, 6)
                        hop(g, (slot - 1) % RING, k)
                    if j in (STAT_MEAN_AT, STAT_VAR_AT) and in_step(0, i + 1):
                        g, nslot = i + 1, (slot + 1) % RING
                        first = j == STAT_MEAN_AT
                        if in_step(0, i - 1):
                            bank_free(i - 1, sum(a < j for a in HOP_AT), None, 0)
                        wait_apart(pe, stat_step, STAT_OPS * g + (2 if first else 5))
                        if first:
                            product(s_mean, k_("avg"), mv[:, nslot, :, 0]).then_inc(stat_mm, 1)
                        else:
                            product(s_var, k_("avg"), var[:]).then_inc(stat_mm, 1)
                    if j % 2 == 0 and in_step(0, i - 2):
                        apply(i - 2, (slot - 2) % RING, j // 2)
                    if j >= QUAD_AT and (j - QUAD_AT) % 2 == 0 and in_step(0, i):
                        q = (j - QUAD_AT) // 2
                        if q < QUADS:
                            turn(i, slot, q)
                        if q > 0:
                            gram(i, q - 1)

            pipeline(pe, step, -1, FULL_LO, FULL_HI, LAST)


_INS = ["x", "L0_conv_weight", "L0_conv_bias"]
_OUTS = [((N, C, 56, 56), "float32")]


def kernel(**inputs):
    import numpy as _np
    import concourse.bacc as _bacc
    from concourse import mybir as _mybir
    from concourse.bass_utils import run_bass_kernel_spmd as _run

    nc = _bacc.Bacc("TRN2", target_bir_lowering=False, num_devices=1)
    arrays, args = {}, []
    for name in _INS:
        a = _np.ascontiguousarray(inputs[name])
        arrays[f"in_{name}_dram"] = a
        args.append(nc.dram_tensor(f"in_{name}_dram", a.shape, _mybir.dt.from_np(a.dtype), kind="ExternalInput").ap())
    a = constants()
    arrays["const_dram"] = a
    args.append(nc.dram_tensor("const_dram", a.shape, _mybir.dt.from_np(a.dtype), kind="ExternalInput").ap())
    for i, (shape, dtype) in enumerate(_OUTS):
        dt = _mybir.dt.from_np(_np.dtype(dtype))
        args.append(nc.dram_tensor(f"out_{i}_dram", shape, dt, kind="ExternalOutput").ap())
    zca_residual(nc, *args)
    r = _run(nc, [arrays], core_ids=[0])
    return r.results[0]["out_0_dram"]
```

```python
from contextlib import ExitStack

import numpy as np

import concourse.bass as bass
from concourse import mybir

ALU = mybir.AluOpType
ACT = mybir.ActivationFunctionType
AX = mybir.AxisListType
F32 = mybir.dt.float32
F16 = mybir.dt.float16

P = 128
N, C, HW = 32, 128, 56 * 56
CG = 8
GROUPS = C // CG
GN = 4
TILES = N * CG // P
SAMPLES = N // TILES
RING = 3
GN_EPS, ZCA_EPS = 1e-5, 1e-4
Y_SCALE = 256.0
TRACE = 8.002

BN = 448
BN_CHUNKS = HW // BN
SPLIT = 784
SPLITS = TILES * HW // SPLIT
LOW = 392
LOWS = TILES * HW // LOW
APPLY = 448
APPLY_CHUNKS = TILES * HW // APPLY
REST = HW % P
QUADS = TILES * (HW // (4 * P)) + 1
QT = HW // (4 * P)
HALF_SLOTS = 28

POLY = [(5.140391, -5.1224), (2.54983, -0.6431659), (2.47836, -0.6337678), (2.319821, -0.6127667),
        (2.036406, -0.5746435), (1.707804, -0.5293551), (1.528766, -0.5040983), (1.500535, -0.5000757)]
ITERS = len(POLY)

HOP_MU, HOP_COV = 0, 1
HOP_M = [None] + [2 * k + 1 for k in range(1, ITERS)]
HOP_YUZ = [2 * k + 2 for k in range(ITERS)]
HOP_T = 2 * ITERS + 1
HOP_V, HOP_ROOT, HOP_TURN = HOP_T + 1, HOP_T + 2, HOP_T + 3
HOPS = HOP_T + 4
READS = HOPS - 1
STAT_OPS = 12
MEAN_OPS = 3
POOL_OPS = 2
TAIL_OPS = 5

HOP_AT = [2] + [3 + k for k in range(1, HOP_TURN)] + [25]
GRAM_READ_AT = 5
STAT_MEAN_AT, STAT_VAR_AT = 13, 15
DVE_LAG = 4
BN_AT = [0, 1, 2, 3, 5, 6, 7, 8, 9, 10, 12, 13, 14, 15]
LOW_AT = [3 + (3 * p) // 2 for p in range(LOWS)]
QUAD_AT = [3 + 2 * q for q in range(QUADS)]

COLS = {}
_at = 0
for _name, _w in (("ident", P), ("avg", P), ("bmask", P), ("ones", P), ("gmask", 64), ("sel", CG),
                  ("e16", 2 * CG), ("expand", P), ("eps", CG), ("eye2", 2 * CG), ("eye15", CG),
                  ("ai", 2 * CG * ITERS)):
    COLS[_name] = (_at, _at + _w)
    _at += _w
CONST_COLS = _at


def constants():
    k = np.zeros((P, CONST_COLS), np.float32)
    p = np.arange(P)

    def put(name, a):
        lo, hi = COLS[name]
        k[:a.shape[0], lo:hi] = a

    put("ident", np.eye(P))
    put("avg", (p[:, None] // GN == p[None] // GN) / GN)
    put("bmask", p[:, None] // CG == p[None] // CG)
    put("ones", np.ones((P, P)))
    ch, part = p // 2, p % 2
    put("gmask", (ch[:, None] // CG == np.arange(64)[None] // CG) * np.where(part == 1, 1.0, 2.0)[:, None]
        / (N * HW * Y_SCALE ** 2))
    put("sel", ch[:, None] % CG == np.arange(CG)[None])
    e = (p[:, None] % CG == np.arange(CG)[None]) / (N * Y_SCALE)
    put("e16", np.concatenate([e, -2.0 * e], 1))
    put("expand", p[None] % CG == np.arange(CG)[:, None])
    eye = np.eye(CG)
    put("eps", eye * (ZCA_EPS / TRACE))
    put("eye2", np.concatenate([eye, eye], 1))
    put("eye15", 1.5 * eye)
    put("ai", np.concatenate([eye * a for a, b in POLY for _ in range(2)], 1))
    return k


def zca_residual(nc: bass.Bass, x: bass.AP, weight: bass.AP, bias: bass.AP, const: bass.AP, out: bass.AP):
    with ExitStack() as ctx:
        def sb(name, shape, dt=F32):
            return ctx.enter_context(nc.sbuf_tensor(name, shape, dt))

        def ps(name, shape, dt=F32):
            return ctx.enter_context(nc.psum_tensor(name, shape, dt))

        def sem(name):
            return ctx.enter_context(nc.semaphore(name))

        x_ring = sb("x_ring", [P, RING, TILES, HW])
        hl_ring = sb("hl_ring", [P, RING, TILES, HW, 2], F16)
        out_buf = sb("out_buf", [P, TILES, HW])
        hl_t = sb("hl_t", [P, 3, 4 * P, 2], F16)
        cst = sb("cst", [P, CONST_COLS])
        wb8 = sb("wb8", [CG, 2, GROUPS])
        wb = sb("wb", [P, GROUPS, 3])
        wb_g = sb("wb_g", [P, RING, 3])
        bn = sb("bn", [P, TILES, BN_CHUNKS, 6])
        mv = sb("mv", [P, RING, TILES, 2])
        dev = sb("dev", [P, RING, TILES])
        var = sb("var", [P, TILES])
        vareps = sb("vareps", [P, TILES])
        root = sb("root", [P, TILES])
        rec = sb("rec", [P, TILES])
        scale = sb("scale", [P, RING, TILES])
        y_mul = sb("y_mul", [P, RING, TILES])
        neg_mean = sb("neg_mean", [P, RING, TILES])
        y_add = sb("y_add", [P, RING, TILES])
        dr = sb("dr", [P, TILES])
        drs = sb("drs", [P, 1])
        e_dr = sb("e_dr", [P, RING, 2 * CG])
        mu = sb("mu", [P, 2 * CG])
        g_masked = sb("g_masked", [P, 64])
        g_red = sb("g_red", [P, CG])
        cov = sb("cov", [CG, CG])
        pp = sb("pp", [CG, 2 * CG])
        yuz = sb("yuz", [CG, 3 * CG])
        tz = sb("tz", [CG, CG])
        res = sb("res", [CG, CG])
        zx = sb("zx", [CG, P])
        rmu = sb("rmu", [P, CG])
        pmu = sb("pmu", [P, 1])
        shift = sb("shift", [P, 1])
        pb = sb("pb", [P, P])
        rw = sb("rw", [P, RING, TILES])
        a_mat = sb("a_mat", [P, TILES, P])
        a_hi = sb("a_hi", [P, RING, TILES, P], F16)
        a_lo = sb("a_lo", [P, RING, TILES, P], F16)
        fin_mul = sb("fin_mul", [P, RING, TILES])
        fin_add = sb("fin_add", [P, RING, TILES])

        ps_apply = ps("ps_apply", [P, 3, 512])
        ps_turn = ps("ps_turn", [P, 2, 512])
        ps_gram = ps("ps_gram", [P, 512])
        ps_small = ps("ps_small", [P, 512])
        ps_stat = ps("ps_stat", [P, 512])

        x_landed = [[sem(f"x_landed_{r}_{s}") for s in range(TILES)] for r in range(RING)]
        out_stored = [sem(f"out_stored_{s}") for s in range(TILES)]
        const_landed = sem("const_landed")
        wb_product = sem("wb_product")
        wb_ready = sem("wb_ready")
        bn_done = sem("bn_done")
        stat_step = sem("stat_step")
        stat_mm = sem("stat_mm")
        root_done = sem("root_done")
        y_ready = sem("y_ready")
        h_ready = sem("h_ready")
        l_ready = sem("l_ready")
        turned = sem("turned")
        turn_copied = sem("turn_copied")
        gram_done = sem("gram_done")
        gram_masked = sem("gram_masked")
        gram_reduced = sem("gram_reduced")
        solve_mm = sem("solve_mm")
        solve_read = sem("solve_read")
        cov_copied = sem("cov_copied")
        res_copied = sem("res_copied")
        tail_step = sem("tail_step")
        a_hi_ready = sem("a_hi_ready")
        a_lo_ready = sem("a_lo_ready")
        applied = sem("applied")
        out_ready = sem("out_ready")
        mean_step = sem("mean_step")
        shift_step = sem("shift_step")
        pool_tail = sem("pool_tail")


        passed = sem("passed")

        x_dram = x.rearrange("(s n) (g c) h w -> g s n c (h w)", s=TILES, c=CG)
        out_dram = out.rearrange("(s n) (g c) h w -> g s n c (h w)", s=TILES, c=CG)

        def k_(name, rows=P):
            lo, hi = COLS[name]
            return cst[0:rows, lo:hi]

        ai = k_("ai", CG)

        s_mu = ps_small[:, 0:16]
        s_cov = ps_small[0:CG, 16:24]
        s_mm = ps_small[0:CG, 24:40]
        s_yuz = ps_small[0:CG, 56:80]
        s_t = ps_small[0:CG, 80:88]
        s_v = ps_small[0:CG, 88:96]
        s_zx = ps_small[0:CG, 96:224]
        s_root = ps_small[:, 224:232]
        s_mean = ps_stat[:, 0:2]
        s_var = ps_stat[:, 2:4]
        s_turn = ps_small[:, 256:512]
        s_wb = ps_small[:, 128:160]

        def wait_apart(eng, semaphore, value):
            eng.wait_ge(semaphore, value)
            eng.sem_inc(passed, 1)

        def ring_of(g, slot, c):
            return (APPLY_CHUNKS * slot + c) % 3

        def in_step(lo, i, hi=GROUPS):
            return not isinstance(i, int) or lo <= i < hi

        def pipeline(eng, step, first, loop_lo, loop_hi, last):
            for i in range(first, loop_lo):
                step(i, i % RING, (i + 1) // RING)
            with eng.Fori(0, (loop_hi - loop_lo) // RING) as trip:
                for u in range(RING):
                    step(trip * RING + (loop_lo + u), (loop_lo + u) % RING, trip + (loop_lo + u + 1) // RING)
            for i in range(loop_hi, last + 1):
                step(i, i % RING, (i + 1) // RING)

        FULL_LO, FULL_HI = 3, 3 + RING * 4
        LAST = GROUPS + 1
        assert FULL_HI + 1 <= GROUPS

        block = ctx.enter_context(nc.Block())

        @block.sync
        def _(sp):
            def load(g, slot, s):
                sp.dma_start(x_ring[:, slot, s, :], x_dram[g, s]).then_inc(x_landed[slot][s], 16)

            for s in range(TILES):
                load(0, 0, s)
            sp.dma_start(cst[:], const).then_inc(const_landed, 16)
            with nc.allow_non_contiguous_dma(reason="256 channel scalars, once"):
                sp.dma_start(wb8[:, 0, :], weight.rearrange("(g j) o -> j (g o)", j=CG)).then_inc(const_landed, 16)
                sp.dma_start(wb8[:, 1, :], bias.rearrange("(g j) o -> j (g o)", j=CG)).then_inc(const_landed, 16)
            for g in range(1, RING):
                for s in range(TILES):
                    load(g, g, s)

            def step(i, slot, visit):
                for s in range(TILES):
                    if in_step(0, i, GROUPS - RING):
                        sp.wait_ge(l_ready, LOWS * i + LOWS // TILES * (s + 1))
                        load(i + RING, slot, s)
                    if in_step(2, i, GROUPS + 2):
                        sp.wait_ge(out_ready, APPLY_CHUNKS * (i - 2) + APPLY_CHUNKS // TILES * (s + 1))
                        sp.dma_start(out_dram[i - 2, s], out_buf[:, s, :]).then_inc(out_stored[s], 16)

            pipeline(sp, step, 0, FULL_LO, FULL_LO + RING * 3, LAST)
            for s in range(TILES):
                sp.wait_ge(out_stored[s], 16 * GROUPS)

        @block.gpsimd
        def _(pool):
            def split(g, slot):
                wait_apart(pool, stat_step, STAT_OPS * (g + 1))
                for a in range(SPLITS + 1):
                    if a < SPLITS:
                        if a % (SPLITS // TILES) == 0 and (not isinstance(g, int) or g >= RING):
                            tiles = a // (SPLITS // TILES) + 1
                            wait_apart(pool, applied, APPLY_CHUNKS * (g - RING) + APPLY_CHUNKS // TILES * tiles)
                        y, h, by, plus = piece(slot, a)
                        nc.gpsimd.tensor_scalar(h, y, by, plus, ALU.mult, ALU.add).then_inc(h_ready, 1)
                    if a > 0:
                        y, h, by, plus = piece(slot, a - 1)
                        wait_apart(pool, h_ready, SPLITS * g + a)
                        nc.gpsimd.tensor_scalar(y, y, by, plus, ALU.mult, ALU.add).then_inc(y_ready, 1)
                    if a < MEAN_OPS:
                        mean_of_channels(g, slot, a)
                    if a == MEAN_OPS and in_step(0, g - 1):
                        tail_begin(g - 1, (slot - 1) % RING)

            def piece(slot, a):
                s, b = divmod(a, SPLITS // TILES)
                px = slice(b * SPLIT, (b + 1) * SPLIT)
                return (x_ring[:, slot, s, px], hl_ring[:, slot, s, px, 1],
                        y_mul[:, slot, s:s + 1], y_add[:, slot, s:s + 1])

            def mean_of_channels(g, slot, a):
                if a > 0:
                    wait_apart(pool, mean_step, MEAN_OPS * g + a)
                if a == 0:
                    ins = nc.gpsimd.tensor_tensor(dr[:], dev[:, slot], y_mul[:, slot], ALU.mult)
                if a == 1:
                    ins = nc.gpsimd.tensor_tensor(drs[:], dr[:, 0:1], dr[:, 1:2], ALU.add)
                if a == 2:
                    ins = nc.gpsimd.tensor_scalar(e_dr[:, slot], k_("e16"), drs[:, 0:1], None, ALU.mult)
                ins.then_inc(mean_step, 1)

            def tail_begin(g, slot):
                nc.gpsimd.tensor_copy(wb_g[:, slot], wb[:, bass.ds(g, 1), :].rearrange("p a b -> p (a b)")).then_inc(pool_tail, 1)
                wait_apart(pool, pool_tail, POOL_OPS * g + 1)
                nc.gpsimd.tensor_scalar(rw[:, slot], y_mul[:, slot], wb_g[:, slot, 1:2], None, ALU.mult).then_inc(pool_tail, 1)

            pool.wait_ge(wb_ready, 1)
            pool.wait_ge(const_landed, 48)

            def step(i, slot, visit):
                if in_step(0, i):
                    split(i, slot)
                elif in_step(0, i - 1):
                    tail_begin(i - 1, (slot - 1) % RING)

            pipeline(pool, step, -1, FULL_LO, FULL_HI, LAST)

        @block.vector
        def _(dve):
            def stats_rows(g, slot):
                wait_apart(dve, bn_done, TILES * BN_CHUNKS * (g + 1))
                for s in range(TILES):
                    nc.vector.bn_aggr(mv[:, slot, s, :], bn[:, s].rearrange("p b k -> p (b k)")).then_inc(stat_step, 1)

            def stats_mean(g, slot):
                dve.wait_ge(stat_mm, 2 * g + 1)
                nc.vector.tensor_tensor(dev[:, slot], mv[:, slot, :, 0], s_mean, ALU.subtract).then_inc(stat_step, 1)
                dve.wait_ge(stat_step, STAT_OPS * g + 3)
                for s in range(TILES):
                    d = dev[:, slot, s:s + 1]
                    nc.vector.scalar_tensor_tensor(out=var[:, s:s + 1], in0=d, scalar=d, in1=mv[:, slot, s, 1:2],
                                                   op0=ALU.mult, op1=ALU.add).then_inc(stat_step, 1)
                nc.vector.tensor_tensor(neg_mean[:, slot], dev[:, slot], mv[:, slot, :, 0],
                                        ALU.subtract).then_inc(stat_step, 1)

            def stats_var(g, slot):
                dve.wait_ge(stat_mm, 2 * g + 2)
                nc.vector.tensor_scalar(vareps[:], s_var, GN_EPS, 0.25 / Y_SCALE ** 2,
                                        ALU.add, ALU.mult).then_inc(stat_step, 1)

            def stats_end(g, slot, part):
                if part == 0:
                    dve.wait_ge(root_done, g + 1)
                    nc.vector.reciprocal(rec[:], root[:]).then_inc(stat_step, 1)
                if part == 1:
                    dve.wait_ge(stat_step, STAT_OPS * g + 8)
                    for s in range(TILES):
                        nc.vector.scalar_tensor_tensor(out=scale[:, slot, s:s + 1], in0=vareps[:, s:s + 1],
                                                       scalar=rec[:, s:s + 1], in1=root[:, s:s + 1],
                                                       op0=ALU.mult, op1=ALU.add).then_inc(stat_step, 1)
                if part == 2:
                    dve.wait_ge(stat_step, STAT_OPS * g + 10)
                    nc.vector.reciprocal(y_mul[:, slot], scale[:, slot]).then_inc(stat_step, 1)
                    dve.wait_ge(stat_step, STAT_OPS * g + 11)
                    nc.vector.tensor_tensor(y_add[:, slot], neg_mean[:, slot], y_mul[:, slot],
                                            ALU.mult).then_inc(stat_step, 1)

            def low_part(g, slot, p):
                if p % (LOWS // SPLITS) == 0:
                    dve.wait_ge(y_ready, SPLITS * g + p // (LOWS // SPLITS) + 1)
                s, b = divmod(p, LOWS // TILES)
                px = slice(b * LOW, (b + 1) * LOW)
                hl = hl_ring[:, slot, s, px]
                nc.vector.tensor_tensor(hl[:, :, 0], x_ring[:, slot, s, px], hl[:, :, 1],
                                        ALU.subtract).then_inc(l_ready, 1)

            def gram_masked_blocks(g):
                dve.wait_ge(gram_done, QUADS * (g + 1))
                nc.vector.tensor_tensor(g_masked[:], ps_gram[:, 0:64], k_("gmask"),
                                        ALU.mult).then_inc(gram_masked, 1)

            def gram_sum(g):
                dve.wait_ge(gram_masked, g + 1)
                nc.vector.tensor_reduce(g_red[:], g_masked[:].rearrange("p (n i) -> p i n", i=CG),
                                        AX.X, ALU.add).then_inc(gram_reduced, 1)

            def read_hop(g, slot, k):
                if k == HOP_COV:
                    dve.wait_ge(solve_mm, HOPS * g + k + 1)
                    nc.vector.scalar_tensor_tensor(out=cov[:], in0=s_cov, scalar=0.5 / TRACE, in1=k_("eps", CG),
                                                   op0=ALU.mult, op1=ALU.add).then_inc(cov_copied, 1)
                    dve.wait_ge(cov_copied, g + 1)
                    twice = cov[:].unsqueeze(1).broadcast_to([CG, 2, CG])
                    nc.vector.tensor_copy(yuz[:, 0:2 * CG].rearrange("p (a b) -> p a b", a=2), twice)
                    nc.vector.tensor_copy(yuz[:, 2 * CG:], k_("eye2", CG)[:, 0:CG])
                    nc.vector.scalar_tensor_tensor(out=pp[:].rearrange("p (a b) -> p a b", a=2), in0=twice,
                                                   scalar=POLY[0][1],
                                                   in1=ai[:, 0:2 * CG].rearrange("p (a b) -> p a b", a=2),
                                                   op0=ALU.mult, op1=ALU.add).then_inc(solve_read, 1)
                if k in HOP_M[1:]:
                    it = HOP_M.index(k)
                    dve.wait_ge(solve_mm, HOPS * g + k + 1)
                    nc.vector.scalar_tensor_tensor(out=pp[:], in0=s_mm, scalar=POLY[it][1],
                                                   in1=ai[:, 2 * CG * it:2 * CG * (it + 1)],
                                                   op0=ALU.mult, op1=ALU.add).then_inc(solve_read, 1)
                if k == HOP_V:
                    dve.wait_ge(solve_mm, HOPS * g + k + 1)
                    nc.vector.scalar_tensor_tensor(out=res[:], in0=s_v, scalar=-0.5, in1=k_("eye15", CG),
                                                   op0=ALU.mult, op1=ALU.add).then_inc(res_copied, 1)
                if k == HOP_ROOT:
                    dve.wait_ge(solve_mm, HOPS * g + k + 1)
                    nc.vector.tensor_tensor(pb[:].rearrange("p (n c) -> p n c", c=CG),
                                            s_root.unsqueeze(1).broadcast_to([P, SAMPLES, CG]),
                                            k_("bmask").rearrange("p (n c) -> p n c", c=CG),
                                            ALU.mult).then_inc(tail_step, 1)
                    nc.vector.tensor_tensor(rmu[:], s_root, mu[:, 0:CG], ALU.mult).then_inc(tail_step, 1)
                    dve.wait_ge(pool_tail, POOL_OPS * g + 2)
                    dve.wait_ge(tail_step, TAIL_OPS * g + 2)
                    for s in range(TILES):
                        nc.vector.scalar_tensor_tensor(out=a_mat[:, s], in0=pb[:], scalar=rw[:, slot, s:s + 1],
                                                       in1=k_("ident"), op0=ALU.mult,
                                                       op1=ALU.add).then_inc(tail_step, 1)
                    nc.vector.tensor_reduce(pmu[:], rmu[:], AX.X, ALU.add).then_inc(tail_step, 1)
                if k == HOP_TURN:
                    dve.wait_ge(a_hi_ready, g + 1)
                    nc.vector.tensor_tensor(a_lo[:, slot].rearrange("p s c -> p (s c)"), s_turn,
                                            a_hi[:, slot].rearrange("p s c -> p (s c)"),
                                            ALU.subtract).then_inc(solve_read, 1)

            dve.wait_ge(wb_product, 1)
            nc.vector.tensor_scalar(wb[:, :, 0], s_wb[:, 0:GROUPS], -1.0 / TRACE ** 0.5, None, ALU.mult)
            nc.vector.tensor_scalar(wb[:, :, 1], s_wb[:, 0:GROUPS], 1.0 / (Y_SCALE * TRACE ** 0.5), None, ALU.mult)
            nc.vector.tensor_copy(wb[:, :, 2], s_wb[:, GROUPS:2 * GROUPS]).then_inc(wb_ready, 1)
            dve.wait_ge(wb_ready, 1)

            def step(i, slot, visit):
                nslot = (slot + 1) % RING
                for j in range(HALF_SLOTS):
                    if j - DVE_LAG in HOP_AT and in_step(0, i - 1):
                        read_hop(i - 1, (slot - 1) % RING, HOP_AT.index(j - DVE_LAG))
                    elif j - DVE_LAG + HALF_SLOTS in HOP_AT and in_step(0, i - 2):
                        read_hop(i - 2, (slot - 2) % RING, HOP_AT.index(j - DVE_LAG + HALF_SLOTS))
                    if in_step(0, i - 1):
                        if j == GRAM_READ_AT:
                            gram_masked_blocks(i - 1)
                        if j == GRAM_READ_AT + 1:
                            gram_sum(i - 1)
                    if j in LOW_AT and in_step(0, i):
                        low_part(i, slot, LOW_AT.index(j))
                    if j in BN_AT and in_step(0, i + 1):
                        s, b = divmod(BN_AT.index(j), BN_CHUNKS)
                        if b == 0:
                            dve.wait_ge(x_landed[nslot][s], 16 * (visit + 1))
                        nc.vector.bn_stats(bn[:, s, b, :],
                                           x_ring[:, nslot, s, b * BN:(b + 1) * BN]).then_inc(bn_done, 1)
                    if in_step(0, i + 1):
                        if j == STAT_MEAN_AT + DVE_LAG - 1:
                            stats_rows(i + 1, nslot)
                        if j == STAT_MEAN_AT + DVE_LAG + 1:
                            stats_mean(i + 1, nslot)
                        if j == STAT_VAR_AT + DVE_LAG + 1:
                            stats_var(i + 1, nslot)
                        if 0 <= j - (STAT_VAR_AT + DVE_LAG + 3) < 3:
                            stats_end(i + 1, nslot, j - (STAT_VAR_AT + DVE_LAG + 3))

            pipeline(dve, step, -1, FULL_LO, FULL_HI, LAST)

        @block.scalar
        def _(act):
            def stats_root(g, slot):
                act.wait_ge(stat_step, STAT_OPS * g + 7)
                nc.scalar.activation(root[:], vareps[:], ACT.Sqrt).then_inc(root_done, 1)

            def copy_turned(g, slot, q):
                act.wait_ge(turned, QUADS * g + q + 1)
                before = q - 3 if q >= 3 else max(b for b in range(QUADS) if b % 3 == q % 3) - QUADS
                if before >= 0 or not isinstance(g, int) or g > 0:
                    act.wait_ge(gram_done, QUADS * g + before + 1)
                rows, cols = (P, 4 * P) if q < QUADS - 1 else (REST, TILES * P)
                dst = hl_t[0:rows, q % 3, 0:cols].rearrange("p c k -> p (c k)").bitcast(F32)
                nc.scalar.copy(dst, ps_turn[0:rows, q % 2, 0:cols]).then_inc(turn_copied, 1)

            def finish(g, slot, c):
                s, b = divmod(c, APPLY_CHUNKS // TILES)
                if b == 0:
                    if s == 0:
                        act.wait_ge(shift_step, 3 * (g + 1))
                    if not isinstance(g, int) or g > 0:
                        act.wait_ge(out_stored[s], 16 * g)
                act.wait_ge(applied, APPLY_CHUNKS * g + c + 1)
                bank = ring_of(g, slot, c)
                nc.scalar.activation(out_buf[:, s, b * APPLY:(b + 1) * APPLY], ps_apply[:, bank, 0:APPLY],
                                     ACT.Identity, bias=fin_add[:, slot, s:s + 1],
                                     scale=fin_mul[:, slot, s:s + 1]).then_inc(out_ready, 1)

            def read_hop(g, slot, k):
                def copy(dst, src):
                    act.wait_ge(solve_mm, HOPS * g + k + 1)
                    nc.scalar.copy(dst, src).then_inc(solve_read, 1)

                if k == HOP_MU:
                    copy(mu[:], s_mu)
                if k in HOP_YUZ[:-1]:
                    copy(yuz[:], s_yuz)
                if k == HOP_YUZ[-1]:
                    copy(yuz[:, 2 * CG:], s_yuz[:, 2 * CG:])
                if k == HOP_T:
                    copy(tz[:], s_t)
                if k == HOP_V:
                    act.wait_ge(res_copied, g + 1)
                    copy(zx[:], s_zx)
                if k == HOP_TURN:
                    act.wait_ge(solve_mm, HOPS * g + k + 1)
                    nc.scalar.copy(a_hi[:, slot].rearrange("p s c -> p (s c)"), s_turn).then_inc(a_hi_ready, 1)
                    act.wait_ge(tail_step, TAIL_OPS * (g + 1))
                    nc.scalar.activation(shift[:], pmu[:], ACT.Identity, bias=wb_g[:, slot, 2:3],
                                         scale=wb_g[:, slot, 0:1]).then_inc(shift_step, 1)
                    nc.scalar.copy(fin_mul[:, slot], scale[:, slot]).then_inc(shift_step, 1)
                    act.wait_ge(shift_step, 3 * g + 1)
                    nc.scalar.activation(fin_add[:, slot], neg_mean[:, slot], ACT.Identity, bias=shift[:],
                                         scale=-1.0).then_inc(shift_step, 1)

            def step(i, slot, visit):
                for j in range(HALF_SLOTS):
                    if j in HOP_AT and in_step(0, i - 1):
                        read_hop(i - 1, (slot - 1) % RING, HOP_AT.index(j))
                    if j == STAT_VAR_AT + 2 and in_step(0, i + 1):
                        stats_root(i + 1, (slot + 1) % RING)
                    if j % 2 == 1 and in_step(0, i - 2):
                        finish(i - 2, (slot - 2) % RING, j // 2)
                    if j - 1 in QUAD_AT and in_step(0, i):
                        copy_turned(i, slot, QUAD_AT.index(j - 1))
                    if j == 0 and in_step(0, i - 1):
                        copy_turned(i - 1, (slot - 1) % RING, QUADS - 1)

            pipeline(act, step, -1, FULL_LO, FULL_HI, LAST)

        @block.tensor
        def _(pe):
            def product(out_, lhsT, rhs, start=True, stop=True):
                return nc.tensor.matmul(out_, lhsT, rhs, start=start, stop=stop, skip_group_check=True)

            def turn(g, slot, q):
                s = min(q // QT, TILES - 1)
                end = min((q - s * QT + 1) * 4 * P, HW) if q < QUADS - 1 else HW
                low = LOWS * g + LOWS // TILES * s + (end - 1) // LOW + 1
                if q < QUADS - 1:
                    pe.wait_ge(l_ready, low)
                else:
                    wait_apart(pe, l_ready, low)
                for b in range(4 if q < QUADS - 1 else TILES):
                    if q < QUADS - 1:
                        s, px, n = q // QT, (q % QT * 4 + b) * P, P
                    else:
                        s, px, n = b, HW - REST, REST
                    words = hl_ring[:, slot, s, px:px + n].rearrange("p c k -> p (c k)").bitcast(F32)
                    ins = nc.tensor.transpose(ps_turn[0:n, q % 2, b * P:(b + 1) * P], words, k_("ident"))
                ins.then_inc(turned, 1)

            def gram(g, q):
                pe.wait_ge(turn_copied, QUADS * g + q + 1)
                if q == 0 and (not isinstance(g, int) or g > 0):
                    pe.wait_ge(gram_masked, g)
                full = q < QUADS - 1
                rows, blocks = (P, 4) if full else (REST, TILES)
                for b in range(blocks):
                    for half in range(2):
                        pair = hl_t[0:rows, q % 3, b * P + half * 64:b * P + half * 64 + 64]
                        first = q == 0 and b == 0 and half == 0
                        last = not full and b == blocks - 1 and half == 1
                        ins = product(ps_gram[:, 0:64], pair.rearrange("p c k -> p (c k)"), pair[:, :, 1],
                                      start=first, stop=last)
                ins.then_inc(gram_done, 1)

            def apply(g, slot, c):
                s, b = divmod(c, APPLY_CHUNKS // TILES)
                if c == 0:
                    pe.wait_ge(solve_read, READS * (g + 1))
                if not isinstance(g, int) or APPLY_CHUNKS * g + c >= 3:
                    pe.wait_ge(out_ready, APPLY_CHUNKS * g + c - 2)
                hl = hl_ring[:, slot, s, b * APPLY:(b + 1) * APPLY]
                dst = ps_apply[:, ring_of(g, slot, c), 0:APPLY]
                product(dst, a_hi[:, slot, s], hl[:, :, 1], True, False)
                product(dst, a_hi[:, slot, s], hl[:, :, 0], False, False)
                product(dst, a_lo[:, slot, s], hl[:, :, 1], False, True).then_inc(applied, 1)

            def hop(g, slot, k):
                y, u, z = yuz[:, 0:CG], yuz[:, CG:2 * CG], yuz[:, 2 * CG:]
                p_, pt = pp[:, 0:CG], pp[:, CG:]
                ins = None
                if k != HOP_TURN and (not isinstance(g, int) or READS * g + k > 0):
                    wait_apart(pe, solve_read, READS * g + k)
                if k == HOP_MU:
                    wait_apart(pe, mean_step, MEAN_OPS * (g + 1))
                    ins = product(s_mu, k_("ones"), e_dr[:, slot])
                if k == HOP_COV:
                    wait_apart(pe, gram_reduced, g + 1)
                    product(s_cov, k_("sel"), g_red[:], True, False)
                    product(s_cov, g_red[:], k_("sel"), False, False)
                    ins = product(s_cov, mu[0:1, 0:CG], mu[0:1, CG:], False, True)
                if k in HOP_M[1:]:
                    product(s_mm[:, 0:CG], z, y)
                    ins = product(s_mm[:, CG:], y, z)
                if k in HOP_YUZ:
                    if k != HOP_YUZ[-1]:
                        product(s_yuz[:, 0:CG], u, p_)
                        product(s_yuz[:, CG:2 * CG], p_, u)
                    ins = product(s_yuz[:, 2 * CG:], pt, z)
                if k == HOP_T:
                    ins = product(s_t, cov[:], z)
                if k == HOP_V:
                    product(s_v, z, tz[:])
                    ins = product(s_zx, z, k_("expand", CG))
                if k == HOP_ROOT:
                    ins = product(s_root, zx[:], res[:])
                if k == HOP_TURN:
                    wait_apart(pe, tail_step, TAIL_OPS * g + 4)
                    for s in range(TILES):
                        ins = nc.tensor.transpose(s_turn[:, s * P:(s + 1) * P], a_mat[:, s], k_("ident"))
                ins.then_inc(solve_mm, 1)

            pe.wait_ge(const_landed, 48)
            product(s_wb, k_("expand", CG), wb8[:].rearrange("p a g -> p (a g)")).then_inc(wb_product, 1)
            pe.wait_ge(wb_ready, 1)

            def step(i, slot, visit):
                for j in range(HALF_SLOTS):
                    if j in HOP_AT and in_step(0, i - 1):
                        hop(i - 1, (slot - 1) % RING, HOP_AT.index(j))
                    if j in (STAT_MEAN_AT, STAT_VAR_AT) and in_step(0, i + 1):
                        g, nslot = i + 1, (slot + 1) % RING
                        if j == STAT_MEAN_AT:
                            wait_apart(pe, stat_step, STAT_OPS * g + 2)
                            product(s_mean, k_("avg"), mv[:, nslot, :, 0]).then_inc(stat_mm, 1)
                        else:
                            wait_apart(pe, stat_step, STAT_OPS * g + 5)
                            product(s_var, k_("avg"), var[:]).then_inc(stat_mm, 1)
                    if j % 2 == 0 and in_step(0, i - 2):
                        apply(i - 2, (slot - 2) % RING, j // 2)
                    if j in QUAD_AT and in_step(0, i):
                        q = QUAD_AT.index(j)
                        turn(i, slot, q)
                        if q > 0:
                            gram(i, q - 1)
                    if j == 1 and in_step(0, i - 1):
                        gram(i - 1, QUADS - 1)

            pipeline(pe, step, -1, FULL_LO, FULL_HI, LAST)


_INS = ["x", "L0_conv_weight", "L0_conv_bias"]
_OUTS = [((N, C, 56, 56), "float32")]


def kernel(**inputs):
    import numpy as _np
    import concourse.bacc as _bacc
    from concourse import mybir as _mybir
    from concourse.bass_utils import run_bass_kernel_spmd as _run

    nc = _bacc.Bacc("TRN2", target_bir_lowering=False, num_devices=1)
    arrays, args = {}, []
    for name in _INS:
        a = _np.ascontiguousarray(inputs[name])
        arrays[f"in_{name}_dram"] = a
        args.append(nc.dram_tensor(f"in_{name}_dram", a.shape, _mybir.dt.from_np(a.dtype), kind="ExternalInput").ap())
    a = constants()
    arrays["const_dram"] = a
    args.append(nc.dram_tensor("const_dram", a.shape, _mybir.dt.from_np(a.dtype), kind="ExternalInput").ap())
    for i, (shape, dtype) in enumerate(_OUTS):
        dt = _mybir.dt.from_np(_np.dtype(dtype))
        args.append(nc.dram_tensor(f"out_{i}_dram", shape, dt, kind="ExternalOutput").ap())
    zca_residual(nc, *args)
    r = _run(nc, [arrays], core_ids=[0])
    return r.results[0]["out_0_dram"]
```

```python
from contextlib import ExitStack

import numpy as np

import concourse.bass as bass
from concourse import mybir

ALU = mybir.AluOpType
ACT = mybir.ActivationFunctionType
AX = mybir.AxisListType
F32 = mybir.dt.float32
F16 = mybir.dt.float16

P = 128
N, C, HW = 32, 128, 56 * 56
CG = 8
GROUPS = C // CG
GN = 4
TILES = N * CG // P
SAMPLES = N // TILES
RING = 3
GN_EPS, ZCA_EPS = 1e-5, 1e-4
Y_SCALE = 256.0
TRACE = 8.002

BN = 448
BN_CHUNKS = HW // BN
SPLIT = 784
SPLITS = TILES * HW // SPLIT
LOW = 392
LOW_TILE = HW // LOW
POOL_LOW = SPLIT
LOWS = TILES * LOW_TILE - POOL_LOW // LOW
APPLY = 448
APPLY_CHUNKS = TILES * HW // APPLY
REST = HW % P
QUADS = TILES * (HW // (4 * P)) + 1
QT = HW // (4 * P)
HALF_SLOTS = 28

POLY = [(5.140391, -5.1224), (2.54983, -0.6431659), (2.47836, -0.6337678), (2.319821, -0.6127667),
        (2.036406, -0.5746435), (1.707804, -0.5293551), (1.528766, -0.5040983), (1.500535, -0.5000757)]
ITERS = len(POLY)

HOP_MU, HOP_COV = 0, 1
HOP_M = [None] + [2 * k + 1 for k in range(1, ITERS)]
HOP_YUZ = [2 * k + 2 for k in range(ITERS)]
HOP_T = 2 * ITERS + 1
HOP_V, HOP_ROOT, HOP_TURN = HOP_T + 1, HOP_T + 2, HOP_T + 3
HOPS = HOP_T + 4
READS = HOPS - 1
STAT_OPS = 12
MEAN_OPS = 3
POOL_OPS = 2
TAIL_OPS = 5

APPLY_AT = [54, 56, 58, 60, 62, 64, 66, 68, 70, 72, 74, 76, 78, 80]
QUAD_AT = [2, 5, 7, 9, 11, 13, 15, 17, 19, 21, 23, 25, 27]
LAST_GRAM_AT = 28
HOP_AT = [30, 32, 33, 34, 35, 36, 37, 38, 39, 40, 41, 42, 43, 44, 45, 46, 47, 48, 49, 50, 53]
STAT_PE_AT = [15, 18]
HOP_ACT_LAG = 0
FINISH_AT = [55, 57, 59, 62, 64, 66, 67, 69, 71, 73, 75, 77, 79, 81]
COPY_AT = [3, 6, 8, 10, 12, 14, 16, 18, 20, 22, 24, 26, 28]
ROOT_AT = 18
DVE_LAG = 5
GRAM_READ_AT = 34
BN_AT = [0, 1, 2, 3, 5, 6, 9, 10, 11, 12, 14, 15, 16, 17]
LOW_AT = [3, 4, 7, 8, 9, 11, 13, 15, 18, 20, 20, 22, 24, 25]
STAT_DVE_AT = [18, 20, 22, 25, 25, 26]

COLS = {}
_at = 0
for _name, _w in (("ident", P), ("avg", P), ("bmask", P), ("ones", P), ("gmask", 64), ("sel", CG),
                  ("e16", 2 * CG), ("expand", P), ("eps", CG), ("eye2", 2 * CG), ("eye15", CG),
                  ("ai", 2 * CG * ITERS)):
    COLS[_name] = (_at, _at + _w)
    _at += _w
CONST_COLS = _at


def constants():
    k = np.zeros((P, CONST_COLS), np.float32)
    p = np.arange(P)

    def put(name, a):
        lo, hi = COLS[name]
        k[:a.shape[0], lo:hi] = a

    put("ident", np.eye(P))
    put("avg", (p[:, None] // GN == p[None] // GN) / GN)
    put("bmask", p[:, None] // CG == p[None] // CG)
    put("ones", np.ones((P, P)))
    ch, part = p // 2, p % 2
    put("gmask", (ch[:, None] // CG == np.arange(64)[None] // CG) * np.where(part == 1, 1.0, 2.0)[:, None]
        / (N * HW * Y_SCALE ** 2))
    put("sel", ch[:, None] % CG == np.arange(CG)[None])
    e = (p[:, None] % CG == np.arange(CG)[None]) / (N * Y_SCALE)
    put("e16", np.concatenate([e, -2.0 * e], 1))
    put("expand", p[None] % CG == np.arange(CG)[:, None])
    eye = np.eye(CG)
    put("eps", eye * (ZCA_EPS / TRACE))
    put("eye2", np.concatenate([eye, eye], 1))
    put("eye15", 1.5 * eye)
    put("ai", np.concatenate([eye * a for a, b in POLY for _ in range(2)], 1))
    return k


def zca_residual(nc: bass.Bass, x: bass.AP, weight: bass.AP, bias: bass.AP, const: bass.AP, out: bass.AP):
    with ExitStack() as ctx:
        def sb(name, shape, dt=F32):
            return ctx.enter_context(nc.sbuf_tensor(name, shape, dt))

        def ps(name, shape, dt=F32):
            return ctx.enter_context(nc.psum_tensor(name, shape, dt))

        def sem(name):
            return ctx.enter_context(nc.semaphore(name))

        x_ring = sb("x_ring", [P, RING, TILES, HW])
        hl_ring = sb("hl_ring", [P, RING, TILES, HW, 2], F16)
        out_buf = sb("out_buf", [P, TILES, HW])
        hl_t = sb("hl_t", [P, 3, 4 * P, 2], F16)
        cst = sb("cst", [P, CONST_COLS])
        wb8 = sb("wb8", [CG, 2, GROUPS])
        wb = sb("wb", [P, GROUPS, 3])
        wb_g = sb("wb_g", [P, RING, 3])
        bn = sb("bn", [P, TILES, BN_CHUNKS, 6])
        mv = sb("mv", [P, RING, TILES, 2])
        dev = sb("dev", [P, RING, TILES])
        var = sb("var", [P, TILES])
        vareps = sb("vareps", [P, TILES])
        root = sb("root", [P, TILES])
        rec = sb("rec", [P, TILES])
        scale = sb("scale", [P, RING, TILES])
        y_mul = sb("y_mul", [P, RING, TILES])
        neg_mean = sb("neg_mean", [P, RING, TILES])
        y_add = sb("y_add", [P, RING, TILES])
        dr = sb("dr", [P, TILES])
        drs = sb("drs", [P, 1])
        e_dr = sb("e_dr", [P, RING, 2 * CG])
        mu = sb("mu", [P, 2 * CG])
        g_masked = sb("g_masked", [P, 64])
        g_red = sb("g_red", [P, CG])
        cov = sb("cov", [CG, CG])
        pp = sb("pp", [CG, 2 * CG])
        yuz = sb("yuz", [CG, 3 * CG])
        tz = sb("tz", [CG, CG])
        res = sb("res", [CG, CG])
        zx = sb("zx", [CG, P])
        rmu = sb("rmu", [P, CG])
        pmu = sb("pmu", [P, 1])
        shift = sb("shift", [P, 1])
        pb = sb("pb", [P, P])
        rw = sb("rw", [P, RING, TILES])
        a_mat = sb("a_mat", [P, TILES, P])
        a_hi = sb("a_hi", [P, RING, TILES, P], F16)
        a_lo = sb("a_lo", [P, RING, TILES, P], F16)
        fin_mul = sb("fin_mul", [P, RING, TILES])
        fin_add = sb("fin_add", [P, RING, TILES])

        ps_apply = ps("ps_apply", [P, 3, 512])
        ps_turn = ps("ps_turn", [P, 2, 512])
        ps_gram = ps("ps_gram", [P, 512])
        ps_small = ps("ps_small", [P, 512])
        ps_stat = ps("ps_stat", [P, 512])

        x_landed = [[sem(f"x_landed_{r}_{s}") for s in range(TILES)] for r in range(RING)]
        out_stored = [sem(f"out_stored_{s}") for s in range(TILES)]
        const_landed = sem("const_landed")
        wb_product = sem("wb_product")
        wb_ready = sem("wb_ready")
        bn_done = sem("bn_done")
        stat_step = sem("stat_step")
        stat_mm = sem("stat_mm")
        root_done = sem("root_done")
        y_ready = sem("y_ready")
        h_ready = sem("h_ready")
        l_ready = sem("l_ready")
        l_pool_ready = sem("l_pool_ready")
        turned = sem("turned")
        turn_copied = sem("turn_copied")
        gram_done = sem("gram_done")
        gram_masked = sem("gram_masked")
        gram_reduced = sem("gram_reduced")
        solve_mm = sem("solve_mm")
        solve_read = sem("solve_read")
        cov_copied = sem("cov_copied")
        res_copied = sem("res_copied")
        tail_step = sem("tail_step")
        a_hi_ready = sem("a_hi_ready")
        a_lo_ready = sem("a_lo_ready")
        applied = sem("applied")
        out_ready = sem("out_ready")
        mean_step = sem("mean_step")
        shift_step = sem("shift_step")
        pool_tail = sem("pool_tail")


        passed = sem("passed")

        x_dram = x.rearrange("(s n) (g c) h w -> g s n c (h w)", s=TILES, c=CG)
        out_dram = out.rearrange("(s n) (g c) h w -> g s n c (h w)", s=TILES, c=CG)

        def k_(name, rows=P):
            lo, hi = COLS[name]
            return cst[0:rows, lo:hi]

        ai = k_("ai", CG)

        s_mu = ps_small[:, 0:16]
        s_cov = ps_small[0:CG, 16:24]
        s_mm = ps_small[0:CG, 24:40]
        s_my, s_mz = ps_small[0:CG, 24:32], ps_small[0:CG, 32:40]
        s_yuz = ps_small[0:CG, 56:80]
        s_y, s_u, s_z = ps_small[0:CG, 56:64], ps_small[0:CG, 64:72], ps_small[0:CG, 72:80]
        s_t = ps_small[0:CG, 80:88]
        s_v = ps_small[0:CG, 88:96]
        s_zx = ps_small[0:CG, 96:224]
        s_root = ps_small[:, 224:232]
        s_mean = ps_stat[:, 0:2]
        s_var = ps_stat[:, 2:4]
        s_turn = ps_small[:, 256:512]
        s_wb = ps_small[:, 128:160]

        def wait_apart(eng, semaphore, value):
            eng.wait_ge(semaphore, value)
            eng.sem_inc(passed, 1)

        def out_tile(g, s):
            if isinstance(g, int) and g == GROUPS - 1:
                return x_ring[:, (g + 1) % RING, s, :]
            return out_buf[:, s, :]

        def ring_of(g, slot, c):
            return (APPLY_CHUNKS * slot + c) % 3

        def in_step(lo, i, hi=GROUPS):
            return not isinstance(i, int) or lo <= i < hi

        def due(places, j):
            return [(k, a // HALF_SLOTS) for k, a in enumerate(places) if a % HALF_SLOTS == j]

        def pipeline(eng, step, first, loop_lo, loop_hi, last):
            for i in range(first, loop_lo):
                step(i, i % RING, (i + 1) // RING)
            with eng.Fori(0, (loop_hi - loop_lo) // RING) as trip:
                for u in range(RING):
                    step(trip * RING + (loop_lo + u), (loop_lo + u) % RING, trip + (loop_lo + u + 1) // RING)
            for i in range(loop_hi, last + 1):
                step(i, i % RING, (i + 1) // RING)

        FULL_LO, FULL_HI = 4, 4 + RING * 3
        LAST = GROUPS + 2
        assert FULL_HI + 1 <= GROUPS

        block = ctx.enter_context(nc.Block())

        @block.sync
        def _(sp):
            def load(g, slot, s):
                sp.dma_start(x_ring[:, slot, s, :], x_dram[g, s]).then_inc(x_landed[slot][s], 16)

            def store_halves(g, s):
                n = APPLY_CHUNKS // TILES
                for lo, hi in ((0, n // 2 + 1), (n // 2 + 1, n)):
                    px = slice(lo * APPLY, hi * APPLY)
                    sp.wait_ge(out_ready, APPLY_CHUNKS * g + n * s + hi)
                    sp.dma_start(out_dram[g, s, :, :, px], out_tile(g, s)[:, px]).then_inc(out_stored[s], 16)

            for s in range(TILES):
                load(0, 0, s)
            sp.dma_start(cst[:], const).then_inc(const_landed, 16)
            with nc.allow_non_contiguous_dma(reason="256 channel scalars, once"):
                sp.dma_start(wb8[:, 0, :], weight.rearrange("(g j) o -> j (g o)", j=CG)).then_inc(const_landed, 16)
                sp.dma_start(wb8[:, 1, :], bias.rearrange("(g j) o -> j (g o)", j=CG)).then_inc(const_landed, 16)
            for g in range(1, RING):
                for s in range(TILES):
                    load(g, g, s)

            def step(i, slot, visit):
                for s in range(TILES):
                    if in_step(0, i, GROUPS - RING):
                        if s == TILES - 1:
                            wait_apart(sp, l_pool_ready, i + 1)
                        sp.wait_ge(l_ready, LOWS * i + min(LOW_TILE * (s + 1), LOWS))
                        load(i + RING, slot, s)
                    if in_step(2, i, GROUPS + 2):
                        if isinstance(i, int) and i - 2 == GROUPS - 1 and s == TILES - 1:
                            store_halves(i - 2, s)
                        else:
                            sp.wait_ge(out_ready, APPLY_CHUNKS * (i - 2) + APPLY_CHUNKS // TILES * (s + 1))
                            sp.dma_start(out_dram[i - 2, s], out_tile(i - 2, s)).then_inc(out_stored[s], 16)

            pipeline(sp, step, 0, FULL_LO, FULL_HI, LAST)
            for s in range(TILES):
                sp.wait_ge(out_stored[s], 16 * GROUPS + (16 if s == TILES - 1 else 0))

        @block.gpsimd
        def _(pool):
            def split(g, slot):
                wait_apart(pool, stat_step, STAT_OPS * (g + 1))
                for a in range(SPLITS + 1):
                    if a < SPLITS:
                        if a % (SPLITS // TILES) == 0 and (not isinstance(g, int) or g >= RING):
                            tiles = a // (SPLITS // TILES) + 1
                            wait_apart(pool, applied, APPLY_CHUNKS * (g - RING) + APPLY_CHUNKS // TILES * tiles)
                        y, h, by, plus = piece(slot, a)
                        nc.gpsimd.tensor_scalar(h, y, by, plus, ALU.mult, ALU.add).then_inc(h_ready, 1)
                    if a > 0:
                        y, h, by, plus = piece(slot, a - 1)
                        wait_apart(pool, h_ready, SPLITS * g + a)
                        nc.gpsimd.tensor_scalar(y, y, by, plus, ALU.mult, ALU.add).then_inc(y_ready, 1)
                    if a == SPLITS:
                        wait_apart(pool, y_ready, SPLITS * (g + 1))
                        nc.gpsimd.tensor_tensor(hl_ring[:, slot, TILES - 1, HW - POOL_LOW:, 0], y, h,
                                                ALU.subtract).then_inc(l_pool_ready, 1)
                    if a < MEAN_OPS:
                        mean_of_channels(g, slot, a)
                    if a == MEAN_OPS and in_step(0, g - 1):
                        tail_begin(g - 1, (slot - 1) % RING)

            def piece(slot, a):
                s, b = divmod(a, SPLITS // TILES)
                px = slice(b * SPLIT, (b + 1) * SPLIT)
                return (x_ring[:, slot, s, px], hl_ring[:, slot, s, px, 1],
                        y_mul[:, slot, s:s + 1], y_add[:, slot, s:s + 1])

            def mean_of_channels(g, slot, a):
                if a > 0:
                    wait_apart(pool, mean_step, MEAN_OPS * g + a)
                if a == 0:
                    ins = nc.gpsimd.tensor_tensor(dr[:], dev[:, slot], y_mul[:, slot], ALU.mult)
                if a == 1:
                    ins = nc.gpsimd.tensor_tensor(drs[:], dr[:, 0:1], dr[:, 1:2], ALU.add)
                if a == 2:
                    ins = nc.gpsimd.tensor_scalar(e_dr[:, slot], k_("e16"), drs[:, 0:1], None, ALU.mult)
                ins.then_inc(mean_step, 1)

            def tail_begin(g, slot):
                nc.gpsimd.tensor_copy(wb_g[:, slot],
                                      wb[:, bass.ds(g, 1), :].rearrange("p a b -> p (a b)")).then_inc(pool_tail, 1)
                wait_apart(pool, pool_tail, POOL_OPS * g + 1)
                nc.gpsimd.tensor_scalar(rw[:, slot], y_mul[:, slot], wb_g[:, slot, 1:2], None,
                                        ALU.mult).then_inc(pool_tail, 1)

            pool.wait_ge(wb_ready, 1)
            pool.wait_ge(const_landed, 48)

            def step(i, slot, visit):
                if in_step(0, i):
                    split(i, slot)
                elif in_step(0, i - 1):
                    tail_begin(i - 1, (slot - 1) % RING)

            pipeline(pool, step, -1, FULL_LO, FULL_HI, LAST)

        @block.vector
        def _(dve):
            def row_stats(g, slot, piece, visit):
                s, b = divmod(piece, BN_CHUNKS)
                if b == 0:
                    dve.wait_ge(x_landed[slot][s], 16 * (visit + 1))
                nc.vector.bn_stats(bn[:, s, b, :],
                                   x_ring[:, slot, s, b * BN:(b + 1) * BN]).then_inc(bn_done, 1)

            def stats_rows(g, slot):
                wait_apart(dve, bn_done, TILES * BN_CHUNKS * (g + 1))
                for s in range(TILES):
                    nc.vector.bn_aggr(mv[:, slot, s, :], bn[:, s].rearrange("p b k -> p (b k)")).then_inc(stat_step, 1)

            def stats_mean(g, slot):
                dve.wait_ge(stat_mm, 2 * g + 1)
                nc.vector.tensor_tensor(dev[:, slot], mv[:, slot, :, 0], s_mean, ALU.subtract).then_inc(stat_step, 1)
                dve.wait_ge(stat_step, STAT_OPS * g + 3)
                for s in range(TILES):
                    d = dev[:, slot, s:s + 1]
                    nc.vector.scalar_tensor_tensor(out=var[:, s:s + 1], in0=d, scalar=d, in1=mv[:, slot, s, 1:2],
                                                   op0=ALU.mult, op1=ALU.add).then_inc(stat_step, 1)
                nc.vector.tensor_tensor(neg_mean[:, slot], dev[:, slot], mv[:, slot, :, 0],
                                        ALU.subtract).then_inc(stat_step, 1)

            def stats_var(g, slot):
                dve.wait_ge(stat_mm, 2 * g + 2)
                nc.vector.tensor_scalar(vareps[:], s_var, GN_EPS, 0.25 / Y_SCALE ** 2,
                                        ALU.add, ALU.mult).then_inc(stat_step, 1)

            def stats_reciprocal(g, slot):
                dve.wait_ge(root_done, g + 1)
                nc.vector.reciprocal(rec[:], root[:]).then_inc(stat_step, 1)

            def stats_heron(g, slot):
                dve.wait_ge(stat_step, STAT_OPS * g + 8)
                for s in range(TILES):
                    nc.vector.scalar_tensor_tensor(out=scale[:, slot, s:s + 1], in0=vareps[:, s:s + 1],
                                                   scalar=rec[:, s:s + 1], in1=root[:, s:s + 1],
                                                   op0=ALU.mult, op1=ALU.add).then_inc(stat_step, 1)

            def stats_scale(g, slot):
                dve.wait_ge(stat_step, STAT_OPS * g + 10)
                nc.vector.reciprocal(y_mul[:, slot], scale[:, slot]).then_inc(stat_step, 1)
                dve.wait_ge(stat_step, STAT_OPS * g + 11)
                nc.vector.tensor_tensor(y_add[:, slot], neg_mean[:, slot], y_mul[:, slot],
                                        ALU.mult).then_inc(stat_step, 1)

            def low_part(g, slot, p):
                if p % (SPLIT // LOW) == 0:
                    dve.wait_ge(y_ready, SPLITS * g + p // (SPLIT // LOW) + 1)
                s, b = divmod(p, LOW_TILE)
                px = slice(b * LOW, (b + 1) * LOW)
                hl = hl_ring[:, slot, s, px]
                nc.vector.tensor_tensor(hl[:, :, 0], x_ring[:, slot, s, px], hl[:, :, 1],
                                        ALU.subtract).then_inc(l_ready, 1)

            def gram_masked_blocks(g):
                dve.wait_ge(gram_done, QUADS * (g + 1))
                nc.vector.tensor_tensor(g_masked[:], ps_gram[:, 0:64], k_("gmask"),
                                        ALU.mult).then_inc(gram_masked, 1)

            def gram_sum(g):
                nc.vector.tensor_copy(yuz[:, 2 * CG:], k_("eye2", CG)[:, 0:CG])
                dve.wait_ge(gram_masked, g + 1)
                nc.vector.tensor_reduce(g_red[:], g_masked[:].rearrange("p (n i) -> p i n", i=CG),
                                        AX.X, ALU.add).then_inc(gram_reduced, 1)

            def read_hop(g, slot, k):
                if k == HOP_COV:
                    dve.wait_ge(solve_mm, HOPS * g + k + 1)
                    def twice(a):
                        return a.unsqueeze(1).broadcast_to([CG, 2, CG])

                    y2 = yuz[:, 0:2 * CG].rearrange("p (a b) -> p a b", a=2)
                    nc.vector.scalar_tensor_tensor(out=y2, in0=twice(s_cov), scalar=0.5 / TRACE,
                                                   in1=twice(k_("eps", CG)), op0=ALU.mult, op1=ALU.add).then_inc(cov_copied, 1)
                    nc.vector.scalar_tensor_tensor(out=cov[:], in0=s_cov, scalar=0.5 / TRACE, in1=k_("eps", CG),
                                                   op0=ALU.mult, op1=ALU.add)
                    dve.wait_ge(cov_copied, g + 1)
                    nc.vector.scalar_tensor_tensor(out=pp[:].rearrange("p (a b) -> p a b", a=2), in0=y2,
                                                   scalar=POLY[0][1],
                                                   in1=ai[:, 0:2 * CG].rearrange("p (a b) -> p a b", a=2),
                                                   op0=ALU.mult, op1=ALU.add).then_inc(solve_read, 1)
                if k in HOP_M[1:]:
                    it = HOP_M.index(k)
                    dve.wait_ge(solve_mm, HOPS * g + k + 1)
                    nc.vector.scalar_tensor_tensor(out=pp[:], in0=s_mm, scalar=POLY[it][1],
                                                   in1=ai[:, 2 * CG * it:2 * CG * (it + 1)],
                                                   op0=ALU.mult, op1=ALU.add).then_inc(solve_read, 1)
                if k == HOP_V:
                    dve.wait_ge(solve_mm, HOPS * g + k + 1)
                    nc.vector.scalar_tensor_tensor(out=res[:], in0=s_v, scalar=-0.5, in1=k_("eye15", CG),
                                                   op0=ALU.mult, op1=ALU.add).then_inc(res_copied, 1)
                if k == HOP_ROOT:
                    dve.wait_ge(solve_mm, HOPS * g + k + 1)
                    nc.vector.tensor_tensor(pb[:].rearrange("p (n c) -> p n c", c=CG),
                                            s_root.unsqueeze(1).broadcast_to([P, SAMPLES, CG]),
                                            k_("bmask").rearrange("p (n c) -> p n c", c=CG),
                                            ALU.mult).then_inc(tail_step, 1)
                    nc.vector.tensor_tensor(rmu[:], s_root, mu[:, 0:CG], ALU.mult).then_inc(tail_step, 1)
                    dve.wait_ge(pool_tail, POOL_OPS * g + 2)
                    dve.wait_ge(tail_step, TAIL_OPS * g + 2)
                    for s in range(TILES):
                        nc.vector.scalar_tensor_tensor(out=a_mat[:, s], in0=pb[:], scalar=rw[:, slot, s:s + 1],
                                                       in1=k_("ident"), op0=ALU.mult,
                                                       op1=ALU.add).then_inc(tail_step, 1)
                    nc.vector.tensor_reduce(pmu[:], rmu[:], AX.X, ALU.add).then_inc(tail_step, 1)
                if k == HOP_TURN:
                    dve.wait_ge(a_hi_ready, g + 1)
                    nc.vector.tensor_tensor(a_lo[:, slot].rearrange("p s c -> p (s c)"), s_turn,
                                            a_hi[:, slot].rearrange("p s c -> p (s c)"),
                                            ALU.subtract).then_inc(solve_read, 1)

            def read_weights():
                dve.wait_ge(wb_product, 1)
                nc.vector.tensor_scalar(wb[:, :, 0], s_wb[:, 0:GROUPS], -1.0 / TRACE ** 0.5, None, ALU.mult)
                nc.vector.tensor_scalar(wb[:, :, 1], s_wb[:, 0:GROUPS], 1.0 / (Y_SCALE * TRACE ** 0.5), None,
                                        ALU.mult)
                nc.vector.tensor_copy(wb[:, :, 2], s_wb[:, GROUPS:2 * GROUPS]).then_inc(wb_ready, 1)

            def step(i, slot, visit):
                for j in range(HALF_SLOTS):
                    for k, back in due([a + DVE_LAG for a in HOP_AT], j):
                        if in_step(0, i - back):
                            read_hop(i - back, (slot - back) % RING, k)
                    for k, back in due([GRAM_READ_AT, GRAM_READ_AT + 1], j):
                        if in_step(0, i - back):
                            (gram_masked_blocks, gram_sum)[k](i - back)
                    for p, back in due(LOW_AT, j):
                        if in_step(0, i - back):
                            low_part(i - back, (slot - back) % RING, p)
                    if in_step(0, i + 1):
                        for b, _ in due(BN_AT, j):
                            row_stats(i + 1, (slot + 1) % RING, b, visit)
                    if isinstance(i, int) and i == -1 and j == BN_AT[-1]:
                        read_weights()
                    for k, back in due(STAT_DVE_AT, j):
                        if in_step(0, i + 1 - back):
                            (stats_rows, stats_mean, stats_var, stats_reciprocal, stats_heron,
                             stats_scale)[k](i + 1 - back, (slot + 1 - back) % RING)

            pipeline(dve, step, -1, FULL_LO, FULL_HI, LAST)

        @block.scalar
        def _(act):
            def stats_root(g, slot):
                act.wait_ge(stat_step, STAT_OPS * g + 7)
                nc.scalar.activation(root[:], vareps[:], ACT.Sqrt).then_inc(root_done, 1)

            def copy_turned(g, slot, q):
                act.wait_ge(turned, QUADS * g + q + 1)
                before = q - 3 if q >= 3 else max(b for b in range(QUADS) if b % 3 == q % 3) - QUADS
                if before >= 0 or not isinstance(g, int) or g > 0:
                    act.wait_ge(gram_done, QUADS * g + before + 1)
                rows, cols = (P, 4 * P) if q < QUADS - 1 else (REST, TILES * P)
                dst = hl_t[0:rows, q % 3, 0:cols].rearrange("p c k -> p (c k)").bitcast(F32)
                nc.scalar.copy(dst, ps_turn[0:rows, q % 2, 0:cols]).then_inc(turn_copied, 1)

            def finish(g, slot, c):
                s, b = divmod(c, APPLY_CHUNKS // TILES)
                if b == 0:
                    if s == 0:
                        act.wait_ge(shift_step, 3 * (g + 1))
                    if not isinstance(g, int) or 0 < g < GROUPS - 1:
                        act.wait_ge(out_stored[s], 16 * g)
                act.wait_ge(applied, APPLY_CHUNKS * g + c + 1)
                bank = ring_of(g, slot, c)
                nc.scalar.activation(out_tile(g, s)[:, b * APPLY:(b + 1) * APPLY], ps_apply[:, bank, 0:APPLY],
                                     ACT.Identity, bias=fin_add[:, slot, s:s + 1],
                                     scale=fin_mul[:, slot, s:s + 1]).then_inc(out_ready, 1)

            def read_hop(g, slot, k):
                def copy(dst, src):
                    act.wait_ge(solve_mm, HOPS * g + k + 1)
                    nc.scalar.copy(dst, src).then_inc(solve_read, 1)

                if k == HOP_MU:
                    copy(mu[:], s_mu)
                if k in HOP_YUZ[:-1]:
                    copy(yuz[:], s_yuz)
                if k == HOP_YUZ[-1]:
                    copy(yuz[:, 2 * CG:], s_yuz[:, 2 * CG:])
                if k == HOP_T:
                    copy(tz[:], s_t)
                if k == HOP_V:
                    act.wait_ge(res_copied, g + 1)
                    copy(zx[:], s_zx)
                if k == HOP_TURN:
                    act.wait_ge(solve_mm, HOPS * g + k + 1)
                    nc.scalar.copy(a_hi[:, slot].rearrange("p s c -> p (s c)"), s_turn).then_inc(a_hi_ready, 1)
                    act.wait_ge(tail_step, TAIL_OPS * (g + 1))
                    nc.scalar.activation(shift[:], pmu[:], ACT.Identity, bias=wb_g[:, slot, 2:3],
                                         scale=wb_g[:, slot, 0:1]).then_inc(shift_step, 1)
                    nc.scalar.copy(fin_mul[:, slot], scale[:, slot]).then_inc(shift_step, 1)
                    act.wait_ge(shift_step, 3 * g + 1)
                    nc.scalar.activation(fin_add[:, slot], neg_mean[:, slot], ACT.Identity, bias=shift[:],
                                         scale=-1.0).then_inc(shift_step, 1)

            def step(i, slot, visit):
                for j in range(HALF_SLOTS):
                    for k, back in due([a + HOP_ACT_LAG for a in HOP_AT], j):
                        if in_step(0, i - back):
                            read_hop(i - back, (slot - back) % RING, k)
                    if j == ROOT_AT and in_step(0, i + 1):
                        stats_root(i + 1, (slot + 1) % RING)
                    for c, back in due(FINISH_AT, j):
                        if in_step(0, i - back):
                            finish(i - back, (slot - back) % RING, c)
                    for q, back in due(COPY_AT, j):
                        if in_step(0, i - back):
                            copy_turned(i - back, (slot - back) % RING, q)

            pipeline(act, step, -1, FULL_LO, FULL_HI, LAST)

        @block.tensor
        def _(pe):
            def product(out_, lhsT, rhs, start=True, stop=True):
                return nc.tensor.matmul(out_, lhsT, rhs, start=start, stop=stop, skip_group_check=True)

            def turn(g, slot, q):
                s = min(q // QT, TILES - 1)
                end = min((q - s * QT + 1) * 4 * P, HW) if q < QUADS - 1 else HW
                low = LOWS * g + min(LOW_TILE * s + (end - 1) // LOW + 1, LOWS)
                if LOW_TILE * s + (end - 1) // LOW + 1 > LOWS:
                    wait_apart(pe, l_pool_ready, g + 1)
                if q < QUADS - 1:
                    pe.wait_ge(l_ready, low)
                else:
                    wait_apart(pe, l_ready, low)
                for b in range(4 if q < QUADS - 1 else TILES):
                    if q < QUADS - 1:
                        s, px, n = q // QT, (q % QT * 4 + b) * P, P
                    else:
                        s, px, n = b, HW - REST, REST
                    words = hl_ring[:, slot, s, px:px + n].rearrange("p c k -> p (c k)").bitcast(F32)
                    ins = nc.tensor.transpose(ps_turn[0:n, q % 2, b * P:(b + 1) * P], words, k_("ident"))
                ins.then_inc(turned, 1)

            def gram(g, q):
                pe.wait_ge(turn_copied, QUADS * g + q + 1)
                if q == 0 and (not isinstance(g, int) or g > 0):
                    pe.wait_ge(gram_masked, g)
                full = q < QUADS - 1
                rows, blocks = (P, 4) if full else (REST, TILES)
                for b in range(blocks):
                    for half in range(2):
                        pair = hl_t[0:rows, q % 3, b * P + half * 64:b * P + half * 64 + 64]
                        first = q == 0 and b == 0 and half == 0
                        last = not full and b == blocks - 1 and half == 1
                        ins = product(ps_gram[:, 0:64], pair.rearrange("p c k -> p (c k)"), pair[:, :, 1],
                                      start=first, stop=last)
                ins.then_inc(gram_done, 1)

            def apply(g, slot, c):
                s, b = divmod(c, APPLY_CHUNKS // TILES)
                if c == 0:
                    pe.wait_ge(solve_read, READS * (g + 1))
                if not isinstance(g, int) or APPLY_CHUNKS * g + c >= 3:
                    pe.wait_ge(out_ready, APPLY_CHUNKS * g + c - 2)
                hl = hl_ring[:, slot, s, b * APPLY:(b + 1) * APPLY]
                dst = ps_apply[:, ring_of(g, slot, c), 0:APPLY]
                product(dst, a_hi[:, slot, s], hl[:, :, 1], True, False)
                product(dst, a_hi[:, slot, s], hl[:, :, 0], False, False)
                product(dst, a_lo[:, slot, s], hl[:, :, 1], False, True).then_inc(applied, 1)

            def mean_average(g, slot):
                pe.wait_ge(stat_step, STAT_OPS * g + 2)
                product(s_mean, k_("avg"), mv[:, slot, :, 0]).then_inc(stat_mm, 1)

            def var_average(g, slot):
                pe.wait_ge(stat_step, STAT_OPS * g + 5)
                product(s_var, k_("avg"), var[:]).then_inc(stat_mm, 1)

            def hop(g, slot, k):
                y, u, z = yuz[:, 0:CG], yuz[:, CG:2 * CG], yuz[:, 2 * CG:]
                p_, pt = pp[:, 0:CG], pp[:, CG:]
                ins = None
                if k != HOP_TURN and (not isinstance(g, int) or READS * g + k > 0):
                    if k in (HOP_MU, HOP_COV, HOP_ROOT):
                        pe.wait_ge(solve_read, READS * g + k)
                    else:
                        wait_apart(pe, solve_read, READS * g + k)
                if k == HOP_MU:
                    pe.wait_ge(mean_step, MEAN_OPS * (g + 1))
                    ins = product(s_mu, k_("ones"), e_dr[:, slot])
                if k == HOP_COV:
                    pe.wait_ge(gram_reduced, g + 1)
                    product(s_cov, k_("sel"), g_red[:], True, False)
                    product(s_cov, g_red[:], k_("sel"), False, False)
                    ins = product(s_cov, mu[0:1, 0:CG], mu[0:1, CG:], False, True)
                if k in HOP_M[1:]:
                    product(s_my, z, y)
                    ins = product(s_mz, y, z)
                if k in HOP_YUZ:
                    if k != HOP_YUZ[-1]:
                        product(s_y, u, p_)
                        product(s_u, p_, u)
                    ins = product(s_z, pt, z)
                if k == HOP_T:
                    ins = product(s_t, cov[:], z)
                if k == HOP_V:
                    product(s_v, z, tz[:])
                    ins = product(s_zx, z, k_("expand", CG))
                if k == HOP_ROOT:
                    ins = product(s_root, zx[:], res[:])
                if k == HOP_TURN:
                    pe.wait_ge(tail_step, TAIL_OPS * g + 4)
                    for s in range(TILES):
                        ins = nc.tensor.transpose(s_turn[:, s * P:(s + 1) * P], a_mat[:, s], k_("ident"))
                ins.then_inc(solve_mm, 1)

            pe.wait_ge(const_landed, 48)
            product(s_wb, k_("expand", CG), wb8[:].rearrange("p a g -> p (a g)")).then_inc(wb_product, 1)
            pe.wait_ge(wb_ready, 1)

            def step(i, slot, visit):
                for j in range(HALF_SLOTS):
                    for k, back in due(HOP_AT, j):
                        if in_step(0, i - back):
                            hop(i - back, (slot - back) % RING, k)
                    if in_step(0, i + 1):
                        for k, _ in due(STAT_PE_AT, j):
                            (mean_average, var_average)[k](i + 1, (slot + 1) % RING)
                    for c, back in due(APPLY_AT, j):
                        if in_step(0, i - back):
                            apply(i - back, (slot - back) % RING, c)
                    for q, back in due(QUAD_AT, j):
                        if in_step(0, i - back):
                            turn(i - back, (slot - back) % RING, q)
                            if q > 0:
                                gram(i - back, q - 1)
                    for _, back in due([LAST_GRAM_AT], j):
                        if in_step(0, i - back):
                            gram(i - back, QUADS - 1)

            pipeline(pe, step, -1, FULL_LO, FULL_HI, LAST)


_INS = ["x", "L0_conv_weight", "L0_conv_bias"]
_OUTS = [((N, C, 56, 56), "float32")]


def kernel(**inputs):
    import numpy as _np
    import concourse.bacc as _bacc
    from concourse import mybir as _mybir
    from concourse.bass_utils import run_bass_kernel_spmd as _run

    nc = _bacc.Bacc("TRN2", target_bir_lowering=False, num_devices=1)
    arrays, args = {}, []
    for name in _INS:
        a = _np.ascontiguousarray(inputs[name])
        arrays[f"in_{name}_dram"] = a
        args.append(nc.dram_tensor(f"in_{name}_dram", a.shape, _mybir.dt.from_np(a.dtype), kind="ExternalInput").ap())
    a = constants()
    arrays["const_dram"] = a
    args.append(nc.dram_tensor("const_dram", a.shape, _mybir.dt.from_np(a.dtype), kind="ExternalInput").ap())
    for i, (shape, dtype) in enumerate(_OUTS):
        dt = _mybir.dt.from_np(_np.dtype(dtype))
        args.append(nc.dram_tensor(f"out_{i}_dram", shape, dt, kind="ExternalOutput").ap())
    zca_residual(nc, *args)
    r = _run(nc, [arrays], core_ids=[0])
    return r.results[0]["out_0_dram"]
```
